# Optimizing a Trainium2 kernel written in Bass

```python
import numpy as np
import jax
import jax.numpy as jnp

def _softmax(x, axis=-1):
    return jax.nn.softmax(x, axis=axis)

def _gelu(x):
    return jax.nn.gelu(x, approximate=True)

def _silu(x):
    return jax.nn.silu(x)

def _sigmoid(x):
    return jax.nn.sigmoid(x)

def _layernorm(x, axis=-1, eps=1e-05):
    m = jnp.mean(x, axis=axis, keepdims=True)
    v = jnp.var(x, axis=axis, keepdims=True)
    return (x - m) / jnp.sqrt(v + eps)

def _scatter_add(tgt, idx, src, axis=0):
    return tgt.at[idx].add(src)

def _segment_sum(src, seg, n):
    return jax.ops.segment_sum(src, seg, n)
kernel_name = 'mk_flamingo_gated_d2_seqx_r8_9604b2'

def setup_inputs(seed: int=0):
    np.random.seed(seed)
    _w = jnp.asarray

    def _rec_inputs():
        import jax
        import jax.numpy as jnp
        _rk = jax.random.key(seed)
        x = -0.0002928 + 1 * jax.random.normal(jax.random.fold_in(_rk, 1), (4, 512, 128), jnp.float32)
        _lenS = 512 - jax.random.randint(jax.random.fold_in(_rk, 7), (4,), 0, max(1, 512 // 4) + 1, jnp.int32)
        _lenS2 = 32 - jax.random.randint(jax.random.fold_in(_rk, 8), (4,), 0, max(1, 32 // 4) + 1, jnp.int32)
        _ctx_1024P = jax.random.normal(jax.random.fold_in(_rk, 11), (4, 16, 128), jnp.float32)
        _ctx_1024c = jax.random.dirichlet(jax.random.fold_in(_rk, 511), 0.3 * jnp.ones((16,), jnp.float32), (4, 32))
        _ctx_1024t = jnp.einsum('bsk,bkd->bsd', _ctx_1024c, _ctx_1024P)
        _ctx_1024t = _ctx_1024t * jax.lax.rsqrt(jnp.mean(jnp.square(_ctx_1024t)) + 1e-12) * 0.953939
        ctx_1024 = -1.39393e-06 + 0.999914 * (_ctx_1024t + 0.3 * jax.random.normal(jax.random.fold_in(_rk, 611), (4, 32, 128), jnp.float32))
        _validS = jnp.arange(512)[None, :] < _lenS[:, None]
        _validS2 = jnp.arange(32)[None, :] < _lenS2[:, None]
        _causal = jnp.tril(jnp.ones((512, 512), dtype=bool))
        mask_BxSxS2_if1 = jnp.where(jnp.ones((4, 512, 32), dtype=bool), 1, 0).astype(jnp.int32)
        mask_BxSxS2_ik0 = jnp.where(jnp.broadcast_to(_validS2[:, None, :], (4, 512, 32)), 0, 1).astype(jnp.int32)
        _g = jax.random.normal(jax.random.fold_in(_rk, 9001), (2, 2), jnp.float32)
        _g = jnp.sign(_g) * jnp.maximum(jnp.abs(_g), 1.0) + (_g == 0) * 1.0
        g_xattn = _g[0]
        g_ffn = _g[1]
        return (x, ctx_1024, mask_BxSxS2_if1, mask_BxSxS2_ik0, g_xattn, g_ffn)
    x, ctx_1024, mask_BxSxS2_if1, mask_BxSxS2_ik0, g_xattn, g_ffn = _rec_inputs()

    def _L0_xattn_setup():
        import jax, jax.numpy as jnp
        import numpy as np
        B, S, E, H = (2, 256, 128, 16)
        DK = E // H
        key = jax.random.key(seed)
        ks = jax.random.split(key, 12)
        scale = 1.0 / np.sqrt(E)
        return {'query': jax.random.normal(ks[0], (B, S, E), jnp.float32), 'key': jax.random.normal(ks[1], (B, S, E), jnp.float32), 'value': jax.random.normal(ks[2], (B, S, E), jnp.float32), 'key_padding_mask': jnp.ones((B, S, S), jnp.int32), 'Wq': jax.random.normal(ks[3], (E, E), jnp.float32) * scale, 'bq': jax.random.normal(ks[4], (E,), jnp.float32) * scale, 'Wk': jax.random.normal(ks[5], (E, E), jnp.float32) * scale, 'bk': jax.random.normal(ks[6], (E,), jnp.float32) * scale, 'Wv': jax.random.normal(ks[7], (E, E), jnp.float32) * scale, 'bv': jax.random.normal(ks[8], (E,), jnp.float32) * scale, 'Wo': jax.random.normal(ks[9], (E, E), jnp.float32) * scale, 'bo': jax.random.normal(ks[10], (E,), jnp.float32) * scale}
    _L0_xattn_all = _L0_xattn_setup()
    _L0_xattn_in = {k: v for k, v in _L0_xattn_all.items() if k in ('Wq', 'bq', 'Wk', 'bk', 'Wv', 'bv', 'Wo', 'bo')}
    del _L0_xattn_all

    def _L0_ffn_setup():
        import jax, jax.numpy as jnp
        import numpy as np
        B, S, H = (4, 256, 128)
        E = 8
        GS = 2
        NG = E // GS
        F = int(H * 4 * (2.0 / 3.0))
        key = jax.random.key(seed)
        ks = jax.random.split(key, 7)
        sc_h = 1.0 / np.sqrt(H)
        sc_f = 1.0 / np.sqrt(F)
        return {'x': jax.random.normal(ks[0], (B, S, H), dtype=jnp.float32), 'Wr': jax.random.normal(ks[1], (H, E), dtype=jnp.float32) * sc_h, 'br': jnp.zeros((E,), dtype=jnp.float32), 'W_up': jax.random.normal(ks[2], (NG, H, F), dtype=jnp.float32) * sc_h, 'b_up': jax.random.normal(ks[3], (NG, F), dtype=jnp.float32) * 0.01, 'W_down': jax.random.normal(ks[4], (E, F, H), dtype=jnp.float32) * sc_f, 'b_down': jax.random.normal(ks[5], (E, H), dtype=jnp.float32) * 0.01}
    _L0_ffn_all = _L0_ffn_setup()
    _L0_ffn_in = {k: v for k, v in _L0_ffn_all.items() if k in ('Wr', 'br', 'W_up', 'b_up', 'W_down', 'b_down')}
    del _L0_ffn_all

    def _L1_xattn_setup():
        import jax, jax.numpy as jnp
        import numpy as np
        B, NKV, NQ, D, H = (4, 256, 128, 128, 16)
        HD = D // H
        key = jax.random.key(seed)
        ks = jax.random.split(key, 9)
        s = 0.02
        return {'x': jax.random.normal(ks[0], (B, NKV, D), jnp.float32), 'y': jax.random.normal(ks[1], (B, NQ, D), jnp.float32), 'mask': jax.random.randint(ks[2], (B, NQ, NKV), 0, 2, jnp.int32), 'W_kv': jax.random.normal(ks[3], (D, 2 * D), jnp.float32) * s, 'b_kv': jnp.zeros((2 * D,), jnp.float32), 'W_q': jax.random.normal(ks[4], (D, D), jnp.float32) * s, 'b_q': jnp.zeros((D,), jnp.float32), 'W_o': jax.random.normal(ks[5], (D, D), jnp.float32) * s, 'b_o': jnp.zeros((D,), jnp.float32)}
    _L1_xattn_all = _L1_xattn_setup()
    _L1_xattn_in = {k: v for k, v in _L1_xattn_all.items() if k in ('W_kv', 'b_kv', 'W_q', 'b_q', 'W_o', 'b_o')}
    del _L1_xattn_all

    def _L1_ffn_setup():
        import jax, jax.numpy as jnp
        import numpy as np
        H_DIM, E_DIM = (128, 64)
        N_SHARED, N_ROUTED, TOP_K = (2, 16, 4)
        B, S = (4, 256)
        key = jax.random.key(seed)
        ks = jax.random.split(key, 6)
        sc = 1.0 / np.sqrt(H_DIM)
        ec = 1.0 / np.sqrt(E_DIM)
        return {'x': jax.random.normal(ks[0], (B, S, H_DIM), dtype=jnp.float32), 'shared_up': jax.random.uniform(ks[1], (N_SHARED, E_DIM, H_DIM), jnp.float32, -sc, sc), 'shared_down': jax.random.uniform(ks[2], (N_SHARED, H_DIM, E_DIM), jnp.float32, -ec, ec), 'routed_up': jax.random.uniform(ks[3], (N_ROUTED, E_DIM, H_DIM), jnp.float32, -sc, sc), 'routed_down': jax.random.uniform(ks[4], (N_ROUTED, H_DIM, E_DIM), jnp.float32, -ec, ec), 'router_w': jax.random.uniform(ks[5], (N_ROUTED, H_DIM), jnp.float32, -sc, sc)}
    _L1_ffn_all = _L1_ffn_setup()
    _L1_ffn_in = {k: v for k, v in _L1_ffn_all.items() if k in ('shared_up', 'shared_down', 'routed_up', 'routed_down', 'router_w')}
    del _L1_ffn_all
    return {'x': x, 'ctx_1024': ctx_1024, 'mask_BxSxS2_if1': mask_BxSxS2_if1, 'mask_BxSxS2_ik0': mask_BxSxS2_ik0, 'g_xattn': g_xattn, 'g_ffn': g_ffn, 'L0_xattn_Wq': _L0_xattn_in['Wq'], 'L0_xattn_bq': _L0_xattn_in['bq'], 'L0_xattn_Wk': _L0_xattn_in['Wk'], 'L0_xattn_bk': _L0_xattn_in['bk'], 'L0_xattn_Wv': _L0_xattn_in['Wv'], 'L0_xattn_bv': _L0_xattn_in['bv'], 'L0_xattn_Wo': _L0_xattn_in['Wo'], 'L0_xattn_bo': _L0_xattn_in['bo'], 'L0_ffn_Wr': _L0_ffn_in['Wr'], 'L0_ffn_br': _L0_ffn_in['br'], 'L0_ffn_W_up': _L0_ffn_in['W_up'], 'L0_ffn_b_up': _L0_ffn_in['b_up'], 'L0_ffn_W_down': _L0_ffn_in['W_down'], 'L0_ffn_b_down': _L0_ffn_in['b_down'], 'L1_xattn_W_kv': _L1_xattn_in['W_kv'], 'L1_xattn_b_kv': _L1_xattn_in['b_kv'], 'L1_xattn_W_q': _L1_xattn_in['W_q'], 'L1_xattn_b_q': _L1_xattn_in['b_q'], 'L1_xattn_W_o': _L1_xattn_in['W_o'], 'L1_xattn_b_o': _L1_xattn_in['b_o'], 'L1_ffn_shared_up': _L1_ffn_in['shared_up'], 'L1_ffn_shared_down': _L1_ffn_in['shared_down'], 'L1_ffn_routed_up': _L1_ffn_in['routed_up'], 'L1_ffn_routed_down': _L1_ffn_in['routed_down'], 'L1_ffn_router_w': _L1_ffn_in['router_w']}

def reference(x, ctx_1024, mask_BxSxS2_if1, mask_BxSxS2_ik0, g_xattn, g_ffn, L0_xattn_Wq, L0_xattn_bq, L0_xattn_Wk, L0_xattn_bk, L0_xattn_Wv, L0_xattn_bv, L0_xattn_Wo, L0_xattn_bo, L0_ffn_Wr, L0_ffn_br, L0_ffn_W_up, L0_ffn_b_up, L0_ffn_W_down, L0_ffn_b_down, L1_xattn_W_kv, L1_xattn_b_kv, L1_xattn_W_q, L1_xattn_b_q, L1_xattn_W_o, L1_xattn_b_o, L1_ffn_shared_up, L1_ffn_shared_down, L1_ffn_routed_up, L1_ffn_routed_down, L1_ffn_router_w):
    import jax
    import jax.numpy as jnp

    def _L0_xattn_ref(query, key, value, key_padding_mask, Wq, bq, Wk, bk, Wv, bv, Wo, bo):
        import jax, jax.numpy as jnp
        import numpy as np
        B, S, E, H = (2, 256, 128, 16)
        DK = E // H
        b = query.shape[0]
        q = (query @ Wq.T + bq).reshape(b, -1, H, DK).transpose(0, 2, 1, 3)
        k = (key @ Wk.T + bk).reshape(b, -1, H, DK).transpose(0, 2, 1, 3)
        v = (value @ Wv.T + bv).reshape(b, -1, H, DK).transpose(0, 2, 1, 3)
        scores = jnp.einsum('bhqd,bhkd->bhqk', q, k) / np.sqrt(DK)
        mask = key_padding_mask[:, None, :, :] == 0
        scores = jnp.where(mask, -jnp.inf, scores)
        attn = jax.nn.softmax(scores, axis=-1)
        attn = jnp.where(mask, 0.0, attn)
        x = jnp.einsum('bhqk,bhkd->bhqd', attn, v)
        x = x.transpose(0, 2, 1, 3).reshape(b, -1, H * DK)
        return x @ Wo.T + bo

    def _L0_ffn_ref(x, Wr, br, W_up, b_up, W_down, b_down):
        import jax, jax.numpy as jnp
        import numpy as np
        B, S, H = (4, 256, 128)
        E = 8
        GS = 2
        NG = E // GS
        F = int(H * 4 * (2.0 / 3.0))
        b, s, h = x.shape
        n_tok = b * s
        k = n_tok // E
        xf = x.reshape(n_tok, h)
        logits = xf @ Wr + br
        Sm = jax.nn.softmax(logits, axis=-1)
        G_t, idx_t = jax.lax.top_k(Sm.T, k)
        G = G_t.T
        idx = idx_t.T
        tokens = xf[idx]
        group = jnp.arange(E) // GS
        Wu = W_up[group]
        bu = b_up[group]
        mid = jax.nn.silu(jnp.einsum('keh,ehf->kef', tokens, Wu) + bu)
        out = jnp.einsum('kef,efh->keh', mid, W_down) + b_down
        y = jnp.zeros_like(xf).at[idx].add(G[..., None] * out)
        return y.reshape(b, s, h)

    def _L1_xattn_ref(x, y, mask, W_kv, b_kv, W_q, b_q, W_o, b_o):
        import jax, jax.numpy as jnp
        import numpy as np
        B, NKV, NQ, D, H = (4, 256, 128, 128, 16)
        HD = D // H
        b, nkv, _ = x.shape
        nq = y.shape[1]
        kv = x @ W_kv + b_kv
        q = y @ W_q + b_q
        kv = kv.reshape(b, nkv, H, 2 * HD).transpose(0, 2, 1, 3)
        q = q.reshape(b, nq, H, HD).transpose(0, 2, 1, 3)
        k, v = (kv[..., :HD], kv[..., HD:])
        scores = jnp.einsum('bhqd,bhkd->bhqk', q, k) / jnp.sqrt(jnp.float32(HD))
        scores = jnp.where(mask[:, None, :, :] == 0, jnp.float32(-1e+20), scores)
        attn = jax.nn.softmax(scores, axis=-1)
        vals = jnp.einsum('bhqk,bhkd->bhqd', attn, v)
        vals = vals.transpose(0, 2, 1, 3).reshape(b, nq, D)
        return vals @ W_o + b_o

    def _L1_ffn_ref(x, shared_up, shared_down, routed_up, routed_down, router_w):
        import jax, jax.numpy as jnp
        import numpy as np
        H_DIM, E_DIM = (128, 64)
        N_SHARED, N_ROUTED, TOP_K = (2, 16, 4)
        B, S = (4, 256)
        b, s, h = x.shape
        xt = x.reshape(-1, h)
        up_s = jnp.einsum('th,seh->tse', xt, shared_up)
        shared = jnp.einsum('tse,she->th', jax.nn.gelu(up_s, approximate=False), shared_down)
        probs = jax.nn.softmax(xt @ router_w.T, axis=-1)
        topk_p, topk_i = jax.lax.top_k(probs, TOP_K)
        gate = jnp.zeros_like(probs).at[jnp.arange(xt.shape[0])[:, None], topk_i].add(topk_p)
        up_r = jnp.einsum('th,reh->tre', xt, routed_up)
        act = jax.nn.gelu(up_r, approximate=False) * gate[:, :, None]
        routed = jnp.einsum('tre,rhe->th', act, routed_down)
        return (shared + routed).reshape(b, s, h)
    x = x + jnp.tanh(g_xattn[0]) * _L0_xattn_ref(_layernorm(x, axis=-1), ctx_1024, ctx_1024, mask_BxSxS2_if1, L0_xattn_Wq, L0_xattn_bq, L0_xattn_Wk, L0_xattn_bk, L0_xattn_Wv, L0_xattn_bv, L0_xattn_Wo, L0_xattn_bo)
    x = x + jnp.tanh(g_ffn[0]) * _L0_ffn_ref(_layernorm(x, axis=-1), L0_ffn_Wr, L0_ffn_br, L0_ffn_W_up, L0_ffn_b_up, L0_ffn_W_down, L0_ffn_b_down)
    x = x + jnp.tanh(g_xattn[1]) * _L1_xattn_ref(ctx_1024, _layernorm(x, axis=-1), mask_BxSxS2_ik0, L1_xattn_W_kv, L1_xattn_b_kv, L1_xattn_W_q, L1_xattn_b_q, L1_xattn_W_o, L1_xattn_b_o)
    x = x + jnp.tanh(g_ffn[1]) * _L1_ffn_ref(_layernorm(x, axis=-1), L1_ffn_shared_up, L1_ffn_shared_down, L1_ffn_routed_up, L1_ffn_routed_down, L1_ffn_router_w)
    return x

_drawn_inputs = setup_inputs


def setup_inputs(seed=0):
    import zlib

    import numpy as np

    out = dict(_drawn_inputs(seed))
    spreads = {'g_ffn': (-1.0, 0.6),
     'L0_ffn_br': (0.0, 0.1),
     'L1_xattn_b_kv': (0.0, 0.41),
     'L1_xattn_b_q': (0.0, 2.0),
     'L1_xattn_b_o': (0.0, 0.1)}
    factors = {'L0_xattn_bq': 2.706,
     'L0_xattn_bk': 64.0,
     'L0_ffn_b_up': 35.364,
     'L0_ffn_b_down': 8.0,
     'L1_xattn_W_q': 64.0}
    for name, (base, spread) in spreads.items():
        noise = np.random.default_rng([zlib.crc32(name.encode()), seed]).standard_normal(out[name].shape)
        drawn = base * np.exp(spread * noise) if base else spread * noise
        out[name] = jnp.asarray(drawn.astype(out[name].dtype))
    for name, factor in factors.items():
        out[name] = (out[name] * factor).astype(out[name].dtype)
    return out
```

```python
from contextlib import ExitStack

import concourse.bass as bass
from concourse import mybir
from concourse.alu_op_type import AluOpType as ALU

ACT = mybir.ActivationFunctionType
F32 = mybir.dt.float32
F32R = mybir.dt.float32r
BF16 = mybir.dt.bfloat16
I32 = mybir.dt.int32
AX_X = mybir.AxisListType.X

B, S, D, SK, H = 4, 512, 128, 32, 16
DK = D // H
TB = S // 128
NT = B * TB
HC = 4
NC = H // HC
E0, NG, FF = 8, 4, 341
TOPK0 = B * S // E0
FCH = [(0, 128), (128, 128), (256, FF - 256)]
NF = len(FCH)
R1, EH, TOP1 = 16, 64, 4
CH1 = R1 * EH // 128 + 1
LN_EPS = 1e-5
MASKED = -float(2 ** 66)
SCALE = float(DK) ** -0.5
BITS = 30
AHEAD = 2

W_COLS = {}
_at = 0
for _n, _w in (("wq0", D), ("wk0", D), ("wv0", D), ("wo0", D), ("ctxT", B * SK), ("wk1", D), ("wv1", D), ("wq1", D),
               ("wo1", D), ("wr0", E0), ("wr1", R1), ("cols", 4), ("rows", 4 * D + E0), ("ident", 128),
               ("same_e", 128), ("before", 128), ("headcol", H), ("ones_blk", 32), ("key32", SK), ("max16", H),
               ("gate16", R1), ("tile16", NT)):
    W_COLS[_n] = (_at, _w)
    _at += _w
NW = _at


TP, PQ, SM0, SM1, ST0, ST1, PV, SU = range(8)
DOWN_BANKS = [(SM0, SM1), (PV, SU)]


def schedule():
    before, after = [("LN", 0, 0)], []
    for s in range(B + 3):
        before += [("Q", 0, s), ("O", 0, s - 2), ("SM", 0, s), ("ST", 0, s - 1), ("NT", 0, s), ("LN", 0, s + 1),
                   ("LN", 1, s - 2), ("PV", 0, s - 1), ("R0", 0, s - 2)]
    for s in range(B + 3):
        after += [("Q", 1, s - 1), ("DN", 0, s), ("SM", 1, s - 1), ("DN", 1, s), ("NT", 1, s - 1), ("ST", 1, s - 1),
                  ("DN", 2, s), ("PV", 1, s - 1), ("DN", 3, s), ("O", 1, s - 1), ("LN", 2, s), ("R1", 1, s - 2),
                  ("UP1", 1, s - 2), ("UP0", 0, s + AHEAD), ("LN", 3, s - 1), ("DN1", 1, s - 2)]
    first = [st for n, st in enumerate(before) if 0 <= st[2] < B and st not in before[:n]]
    second = [st for st in after if 0 <= st[2] < B]
    return first, second


def bank_uses(first, second):
    uses = {k: {} for k in range(8)}

    def use(k, *key):
        uses[k][key] = len(uses[k])

    for layer in range(2):
        use(PQ, "K", layer)
        use(SM0, "V", layer)
    for name, a, b in first + [("SEL", 0, 0)] + second:
        if name == "LN":
            use(TP, name, a, b)
        elif name in ("Q", "O"):
            use(PQ, name, a, b)
        elif name == "R0":
            use(PQ, name, b)
        elif name == "SM":
            for j in range(TB):
                use(SM0 + j % 2, name, a, b, j)
        elif name == "NT":
            use(TP, name, a, b)
        elif name == "ST":
            for c in range(NC):
                use(ST0 + c % 2, name, a, b, c)
        elif name == "PV":
            use(PV, name, a, b)
            use(SU, name, a, b)
        elif name == "SEL":
            use(TP, "P")
            for i in range(BITS + 1):
                use(PQ, "COUNT", i)
            use(TP, "G")
            for ub in range(AHEAD):
                for i in range(NG * NF):
                    use(ST0 + i % 2, "UP0", ub, i)
        elif name == "UP0":
            for i in range(NG * NF):
                use(ST0 + i % 2, "UP0", b, i)
        elif name == "DN":
            t = TB * b + a
            for k in DOWN_BANKS[t % 2]:
                use(k, "DN", t)
            use(PQ, "BD", t)
        elif name == "R1":
            use(PQ, name, b)
            use(TP, name, b)
        elif name == "UP1":
            for c in range(CH1):
                use(ST0 + c % 2, name, b, c)
                if c < CH1 - 1:
                    use(SM0 + c % 2, "GATE", b, c)
        elif name == "DN1":
            use(PV, name, b)
    return uses


def spread(ap, axis, n):
    ap = ap.unsqueeze(axis)
    shape = list(ap.shape)
    shape[axis] = n
    return ap.broadcast_to(shape)


def build(nc, x, mask_tm, mask_t, weights, gates, w_up, b_up, w_down, b_down, w_up1, w_dn1, out):
    first, second = schedule()
    uses = bank_uses(first, second)
    order = first + second
    nth_ln = {(a, b): n for n, (a, b) in enumerate([(a, b) for name, a, b in order if name == "LN"])}
    nth_att = {(a, b): n for n, (a, b) in enumerate([(a, b) for name, a, b in order if name == "Q"])}
    att = list(nth_att)

    with ExitStack() as ctx:
        def sb(name, shape, dt=F32):
            return ctx.enter_context(nc.sbuf_tensor(name, shape, dt))

        def sem(name):
            return ctx.enter_context(nc.semaphore(name))

        bank = [ctx.enter_context(nc.psum_tensor(f"bank{i}", [128, 512], F32)) for i in range(8)]

        W = sb("W", [128, NW])
        g_raw, g_tanh = sb("g_raw", [128, 4]), sb("g_tanh", [128, 4])
        wup, bup = sb("wup", [128, NG, FF]), sb("bup", [128, NG, NF])
        wdn = sb("wdn", [128, NF, E0, D])
        bdn, bdn_t = sb("bdn", [128, D]), sb("bdn_t", [128, NT, D])
        wup1, wdn1 = sb("wup1", [128, CH1 * 128]), sb("wdn1", [128, CH1, D])
        bk_s = sb("bk_s", [128, 2])
        ident_b = sb("ident_b", [128, 128], BF16)
        same_b, before_b = sb("same_b", [128, 128], BF16), sb("before_b", [128, 128], BF16)
        mask_rows, max_rows = sb("mask_rows", [128, H, SK], BF16), sb("max_rows", [128, H, SK], BF16)
        gate_rows = sb("gate_rows", [128, R1, EH], BF16)
        ctx4, ones_row = sb("ctx4", [128, B, 128]), sb("ones_row", [1, 128])
        any_keep = sb("any_keep", [128, NT])
        X, XB = sb("X", [128, NT, D]), sb("XB", [128, 2, TB, D])
        XN, XT = sb("XN", [128, 2, TB, D]), sb("XT", [128, B, S])
        stats, mv = sb("stats", [128, NT, 6]), sb("mv", [128, NT, 2])
        vare, rstd, minus_half = sb("vare", [128, NT]), sb("rstd", [128, NT]), sb("minus_half", [128, TB])
        QT, QR = sb("QT", [128, 2, S]), sb("QR", [128, 2, S], F32R)
        kcol = sb("kcol", [128, 2, B * SK])
        KB, KR = sb("KB", [128, B, H * SK]), sb("KR", [128, B, H * SK], F32R)
        VB = sb("VB", [128, 2, B * NC, 32])
        shift = sb("shift", [128, B, S], BF16)
        mx, nm = sb("mx", [128, NT, H]), sb("nm", [128, 2, TB, 2, H], BF16)
        PT = sb("PT", [128, 2, NC, S])
        rsum, AT = sb("rsum", [128, S]), sb("AT", [128, 2, S])
        LG, P0 = sb("LG", [128, NT, E0]), sb("P0", [128, NT, E0])
        lmax, lsm, lrc = sb("lmax", [128, NT]), sb("lsm", [128, NT]), sb("lrc", [128, NT])
        PRT, GT = sb("PRT", [128, 128]), sb("GT", [128, 128])
        eq, run, gt = (sb(n, [128, 128]) for n in ("eq", "run", "gt"))
        count, left = sb("count", [128, 2], BF16), sb("left", [128, 2])
        cand, over = sb("cand", [128, 1], I32), sb("over", [128, 1], I32)
        G0 = sb("G0", [128, NT, E0])
        MID = sb("MID", [128, NG * NF, AHEAD, S])
        acc = sb("acc", [128, 2, D])
        lg1, p1 = sb("lg1", [128, TB, R1]), sb("p1", [128, TB, R1 + 4])
        m1, s1, r1 = sb("m1", [128, TB]), sb("s1", [128, TB]), sb("r1", [128, TB])
        top8, take8 = sb("top8", [128, TB, 8]), sb("take8", [128, TB, 8])
        rest, gate = sb("rest", [128, TB, R1 + 4]), sb("gate", [128, TB, R1])
        gres, g3 = sb("gres", [128, TB, R1]), sb("g3", [128, TB, 3, R1], BF16)
        gT = sb("gT", [128, S], BF16)
        HG = sb("HG", [128, CH1, S])
        mask_i = HG[:, 0:B, :].rearrange("p b s -> p (b s)").bitcast(I32)
        keep_i = HG[:, B, :].rearrange("p (t k) -> p t k", t=NT).bitcast(I32)
        keep_f = HG[:, B + 1, :].rearrange("p (t k) -> p t k", t=NT)

        def w(name):
            at, n = W_COLS[name]
            return W[:, at:at + n]

        cols, rows, ident = w("cols"), w("rows"), w("ident")
        wo = [w("wo0"), w("wo1")]
        bo_g = [rows[:, D * layer:D * layer + D] for layer in range(2)]
        bv = [rows[0:1, 2 * D + E0 + D * layer:3 * D + E0 + D * layer] for layer in range(2)]
        x_dram = x.rearrange("(t p) h -> p t h", p=128)
        out_dram = out.rearrange("(t p) h -> p t h", p=128)

        filled = [sem(f"bank{i}_filled") for i in range(8)]
        read_out = [sem(f"bank{i}_read_out") for i in range(8)]

        def may_fill(eng, k, *key):
            if uses[k][key] > 0:
                eng.wait_ge(read_out[k], uses[k][key])

        def is_full(eng, k, *key):
            eng.wait_ge(filled[k], uses[k][key] + 1)

        def is_read(eng, k, *key):
            eng.wait_ge(read_out[k], uses[k][key] + 1)

        x_in = [sem(f"x_in{b}") for b in range(B)]
        w_in, g_in, keep_in, up_in, up1_in = (sem(n) for n in ("w_in", "g_in", "keep_in", "up_in", "up1_in"))
        mask_in = [sem("mask_in0"), sem("mask_in1")]
        dn_in = sem("dn_in")
        tanh_done, mask_done = sem("tanh_done"), [sem("mask_done0"), sem("mask_done1")]
        pool_const, pool_chain, vec_const = sem("pool_const"), sem("pool_chain"), sem("vec_const")
        var_done, rstd_done, xn_done = sem("var_done"), sem("rstd_done"), sem("xn_done")
        kb_done = [sem("kb_done0"), sem("kb_done1")]
        kr_done = sem("kr_done")
        qr_done, nm_done = sem("qr_done"), sem("nm_done")
        rs_done, xb_done = sem("rs_done"), sem("xb_done")
        vec_chain = sem("vec_chain")
        lgs_done, e0_done, count_done = sem("lgs_done"), sem("e0_done"), sem("count_done")
        prob_done, gt_done, bdn_done = sem("prob_done"), sem("gt_done"), sem("bdn_done")
        e1_done, g3_done = sem("e1_done"), sem("g3_done")
        y_out = sem("y_out")

        HALF, BK, MASK_ROWS, MAX_ROWS, WO, BO, GATE_ROWS, WDN1, TAKE = range(1, 10)

        block = ctx.enter_context(nc.Block())

        @block.sync
        def _(sp):
            sp.dma_start(W[:], weights).then_inc(w_in, 16)
            for b in range(B):
                t = slice(TB * b, TB * b + TB)
                sp.dma_start(X[:, t, :], x_dram[:, t, :]).then_inc(x_in[b], 16)
            sp.dma_start(mask_i[64:96, :], mask_t[0]).then_inc(mask_in[0], 16)
            sp.dma_start(keep_i[:], mask_tm.rearrange("(t p) k -> p t k", p=128)).then_inc(keep_in, 16)
            sp.dma_start(wup[:], w_up.rearrange("g h f -> h g f")).then_inc(up_in, 16)
            sp.dma_start(bup[:], b_up).then_inc(up_in, 16)
            sp.dma_start(bdn[:], b_down).then_inc(dn_in, 16)
            for k, (f0, fn) in enumerate(FCH):
                sp.dma_start(wdn[0:fn, k, :, :], w_down[:, f0:f0 + fn, :].rearrange("e f h -> f e h"))\
                    .then_inc(dn_in, 16)
            sp.dma_start(wup1[:], w_up1).then_inc(up1_in, 16)
            sp.dma_start(wdn1[:], w_dn1).then_inc(up1_in, 16)
            sp.wait_ge(mask_done[0], 1)
            sp.dma_start(mask_i[64:96, :], mask_t[1]).then_inc(mask_in[1], 16)
            for b in range(B):
                is_read(sp, PV, "DN1", b)
                t = slice(TB * b, TB * b + TB)
                sp.dma_start(out_dram[:, t, :], X[:, t, :]).then_inc(y_out, 16)
            sp.wait_ge(y_out, 16 * B)

        @block.gpsimd
        def _(pool):
            links = [0]

            def link(ins):
                links[0] += 1
                ins.then_inc(pool_chain, 1)
                pool.wait_ge(pool_chain, links[0])

            def mask_to_rows(layer):
                pool.wait_ge(mask_in[layer], 16)
                if layer == 1:
                    is_read(pool, ST1, "ST", 0, B - 1, NC - 1)
                if layer == 0:
                    pool.wait_ge(pool_const, MASK_ROWS)
                pool.tensor_scalar(shift[64:96, :, :].rearrange("p b s -> p (b s)"), mask_i[64:96, :], 0.0, MASKED,
                                   ALU.is_equal, ALU.mult).then_inc(mask_done[layer], 1)
                pool.wait_ge(mask_done[layer], 1)

            def rstd_of(a, b):
                t = slice(TB * b, TB * b + TB)
                pool.wait_ge(var_done, nth_ln[(a, b)] + 1)
                link(pool.tensor_scalar(vare[:, t], mv[:, t, 1], LN_EPS, None, ALU.add))
                pool.tensor_tensor(rstd[:, t], vare[:, t], minus_half[:], ALU.pow).then_inc(rstd_done, 1)

            def x_plus_bias(layer, b):
                if layer == 0:
                    pool.wait_ge(x_in[b], 16)
                else:
                    is_read(pool, PQ, "BD", TB * b + TB - 1)
                n = nth_att[(layer, b)]
                if n >= 2:
                    is_read(pool, PQ, "O", *att[n - 2])
                pool.tensor_tensor(XB[:, n % 2, :, :], X[:, TB * b:TB * b + TB, :], spread(bo_g[layer], 1, TB),
                                   ALU.add).then_inc(xb_done, 1)

            pool.memset(minus_half[:], -0.5).then_inc(pool_const, 1)
            link(pool.memset(shift[:], 0.0))
            pool.wait_ge(w_in, 16)
            pool.tensor_scalar(bk_s[:], cols[:, 1:4:2], SCALE, None, ALU.mult).then_inc(pool_const, 1)
            rstd_of(0, 0)
            pool.tensor_copy(mask_rows[:], spread(w("key32"), 1, H)).then_inc(pool_const, 1)
            mask_to_rows(0)
            pool.tensor_copy(max_rows[:], spread(w("max16"), 2, SK)).then_inc(pool_const, 1)
            pool.wait_ge(tanh_done, 1)
            pool.tensor_scalar(wo[0], wo[0], g_tanh[:, 0:1], None, ALU.mult)
            pool.tensor_scalar(wo[1], wo[1], g_tanh[:, 2:3], None, ALU.mult).then_inc(pool_const, 1)
            pool.tensor_scalar(bo_g[0], bo_g[0], g_tanh[:, 0:1], None, ALU.mult)
            pool.tensor_scalar(bo_g[1], bo_g[1], g_tanh[:, 2:3], None, ALU.mult).then_inc(pool_const, 1)
            pool.wait_ge(pool_const, BO)

            for name, a, b in first:
                if name == "LN" and (a, b) != (0, 0):
                    rstd_of(a, b)
                if name == "Q":
                    x_plus_bias(0, b)
            is_read(pool, PQ, "K", 1)
            is_read(pool, ST1, "ST", 0, B - 1, NC - 1)
            for b in range(B):
                ins = pool.tensor_tensor(KB[:, b, :].rearrange("p (h k) -> p h k", h=H), spread(w("headcol"), 2, SK),
                                         spread(kcol[:, 1, SK * b:SK * b + SK], 1, H), ALU.mult)
            ins.then_inc(kb_done[1], 1)
            pool.wait_ge(dn_in, 16 * (1 + NF))
            link(pool.tensor_scalar(bdn[:], bdn[:], g_tanh[:, 1:2], None, ALU.mult))
            pool.tensor_tensor(bdn_t[:], spread(bdn[:], 1, NT), spread(w("tile16"), 2, D), ALU.mult)\
                .then_inc(bdn_done, 1)
            pool.wait_ge(bdn_done, 1)
            mask_to_rows(1)
            pool.tensor_copy(gate_rows[:], spread(w("gate16"), 2, EH)).then_inc(pool_const, 1)
            pool.wait_ge(up1_in, 32)
            pool.tensor_scalar(wdn1[:].rearrange("p c h -> p (c h)"), wdn1[:].rearrange("p c h -> p (c h)"),
                               g_tanh[:, 3:4], None, ALU.mult).then_inc(pool_const, 1)
            pool.memset(take8[:], -1.0)
            pool.memset(p1[:], -1.0).then_inc(pool_const, 1)
            for name, a, b in second:
                if name == "LN":
                    rstd_of(a, b)
                    if a == 2:
                        x_plus_bias(1, b)

        @block.scalar
        def _(act):
            act.dma_start(g_raw[:], gates).then_inc(g_in, 16)
            act.wait_ge(g_in, 16)
            act.activation(g_tanh[:], g_raw[:], ACT.Tanh).then_inc(tanh_done, 1)
            act.preload_act_table_set("natural_log_exp_and_others")
            act.wait_ge(pool_const, BK)
            for layer in range(2):
                is_full(act, PQ, "K", layer)
                act.activation(kcol[:, layer, :], bank[PQ][:, 0:B * SK], ACT.Identity, bias=bk_s[:, layer:layer + 1],
                               scale=SCALE).then_inc(read_out[PQ], 1)

            def normalised(a, b):
                is_full(act, TP, "LN", a, b)
                act.activation(XT[:, b, :], bank[TP][:], ACT.Copy).then_inc(read_out[TP], 1)

            def queries(layer, b):
                is_full(act, PQ, "Q", layer, b)
                act.activation(QT[:, nth_att[(layer, b)] % 2, :], bank[PQ][:], ACT.Identity,
                               bias=cols[:, 2 * layer:2 * layer + 1]).then_inc(read_out[PQ], 1)

            def exps(layer, b):
                n = nth_att[(layer, b)]
                if n >= 2:
                    is_full(act, SU, "PV", *att[n - 2])
                for c in range(NC):
                    k = ST0 + c % 2
                    is_full(act, k, "ST", layer, b, c)
                    act.activation(PT[:, n % 2, c, :], bank[k][:], ACT.Exp).then_inc(read_out[k], 1)

            def inverse_sums(layer, b):
                n = nth_att[(layer, b)]
                is_full(act, SU, "PV", layer, b)
                if n >= 1:
                    is_read(act, PV, "PV", *att[n - 1])
                act.activation(rsum[:], bank[SU][:], ACT.Ln).then_inc(read_out[SU], 1)
                is_read(act, SU, "PV", layer, b)
                act.activation(rsum[:], rsum[:], ACT.Exp, scale=-1.0).then_inc(rs_done, 1)

            def hidden0(b, i):
                g, (f0, fn) = i // NF, FCH[i % NF]
                if b >= AHEAD and i == 0:
                    is_full(act, DOWN_BANKS[1][1], "DN", TB * (b - AHEAD) + TB - 1)
                k = ST0 + i % 2
                is_full(act, k, "UP0", b, i)
                act.activation(MID[0:fn, i, b % AHEAD, :], bank[k][0:fn, :], ACT.Silu,
                               bias=bup[0:fn, g, i % NF:i % NF + 1]).then_inc(read_out[k], 1)

            for name, a, b in first:
                if name == "LN":
                    normalised(a, b)
                elif name == "Q":
                    queries(a, b)
                elif name == "ST":
                    exps(a, b)
                elif name == "PV":
                    inverse_sums(a, b)
            act.wait_ge(lgs_done, 1)
            act.activation(P0[:].rearrange("p t e -> p (t e)"), LG[:].rearrange("p t e -> p (t e)"), ACT.Exp)\
                .then_inc(e0_done, 1)
            act.wait_ge(up_in, 32)
            for b in range(AHEAD):
                for i in range(NG * NF):
                    hidden0(b, i)
            for name, a, b in second:
                if name == "LN":
                    normalised(a, b)
                elif name == "Q":
                    queries(a, b)
                elif name == "ST":
                    exps(a, b)
                elif name == "PV":
                    inverse_sums(a, b)
                elif name == "UP0":
                    for i in range(NG * NF):
                        hidden0(b, i)
                elif name == "R1":
                    is_read(act, PQ, "R1", b)
                    act.activation(p1[:, :, 0:R1], lg1[:], ACT.Exp).then_inc(e1_done, 1)
                elif name == "UP1":
                    for c in range(CH1):
                        k = ST0 + c % 2
                        is_full(act, k, "UP1", b, c)
                        if b == 0 and c == 0:
                            act.wait_ge(mask_done[1], 1)
                        if b >= 1 and c == 0:
                            is_full(act, PV, "DN1", b - 1)
                        act.activation(HG[:, c, :], bank[k][:], ACT.Gelu).then_inc(read_out[k], 1)

        @block.tensor
        def _(pe):
            def fill(k):
                return lambda ins: ins.then_inc(filled[k], 1)

            def turn(a, b):
                may_fill(pe, TP, "LN", a, b)
                n = nth_ln[(a, b)]
                pe.wait_ge(xn_done, n + 1)
                for j in range(TB):
                    ins = pe.transpose(bank[TP][:, 128 * j:128 * j + 128], XN[:, n % 2, j, :], ident)
                fill(TP)(ins)

            def keys_values(layer):
                may_fill(pe, PQ, "K", layer)
                fill(PQ)(pe.matmul(bank[PQ][:, 0:B * SK], w(f"wk{layer}"), w("ctxT"), start=True, stop=True))
                may_fill(pe, SM0, "V", layer)
                if layer == 0:
                    pe.wait_ge(vec_const, 1)
                for b in range(B):
                    o = bank[SM0][:, D * b:D * b + D]
                    pe.matmul(o, ctx4[:, b, :], w(f"wv{layer}"), start=True, stop=False)
                    ins = pe.matmul(o, ones_row[:], bv[layer], start=False, stop=True)
                fill(SM0)(ins)

            def queries(layer, b):
                may_fill(pe, PQ, "Q", layer, b)
                is_read(pe, TP, "LN", 2 * layer, b)
                fill(PQ)(pe.matmul(bank[PQ][:], w(f"wq{layer}"), XT[:, b, :], start=True, stop=True))

            def scores_for_max(layer, b):
                n = nth_att[(layer, b)]
                pe.wait_ge(qr_done, n + 1)
                if b == 0:
                    pe.wait_ge(kr_done, layer + 1)
                    pe.wait_ge(mask_done[layer], 1)
                    pe.wait_ge(pool_const, MASK_ROWS)
                for j in range(TB):
                    k = SM0 + j % 2
                    may_fill(pe, k, "SM", layer, b, j)
                    t = slice(128 * j, 128 * j + 128)
                    pe.matmul(bank[k][:], QR[:, n % 2, t], KR[:, b, :], start=True, stop=False)
                    fill(k)(pe.matmul(bank[k][:], shift[:, b, t], mask_rows[:].rearrange("p h k -> p (h k)"),
                                      start=False, stop=True))

            def turn_max(layer, b):
                n = nth_att[(layer, b)]
                may_fill(pe, TP, "NT", layer, b)
                pe.wait_ge(nm_done, n + 1)
                pe.wait_ge(vec_const, 2)
                o = bank[TP][:].bitcast(BF16)
                for j in range(TB):
                    ins = pe.transpose(o[0:2 * H, 128 * j:128 * j + 128],
                                       nm[:, n % 2, j, :, :].rearrange("p a h -> p (a h)"), ident_b[:])
                fill(TP)(ins)

            def scores(layer, b):
                n = nth_att[(layer, b)]
                is_read(pe, TP, "NT", layer, b)
                is_read(pe, PQ, "Q", layer, b)
                if b == 0:
                    pe.wait_ge(kb_done[layer], 1)
                    pe.wait_ge(pool_const, MAX_ROWS)
                for c in range(NC):
                    k = ST0 + c % 2
                    may_fill(pe, k, "ST", layer, b, c)
                    r = slice(128 * c, 128 * c + 128)
                    pe.matmul(bank[k][:], KB[:, b, r], QT[:, n % 2, :], start=True, stop=False)
                    pe.matmul(bank[k][:], mask_rows[:].rearrange("p h k -> p (h k)")[:, r], shift[:, b, :],
                              start=False, stop=False)
                    fill(k)(pe.matmul(bank[k][:], max_rows[:].rearrange("p h k -> p (h k)")[:, r], shift[:, b, :],
                                      start=False, stop=True))

            def attend(layer, b):
                n = nth_att[(layer, b)]
                may_fill(pe, PV, "PV", layer, b)
                may_fill(pe, SU, "PV", layer, b)
                is_read(pe, SM0, "V", layer)
                is_read(pe, ST0, "ST", layer, b, NC - 2)
                is_read(pe, ST1, "ST", layer, b, NC - 1)
                for c in range(NC):
                    ins = pe.matmul(bank[PV][32 * c:32 * c + 32, :], VB[:, layer, NC * b + c, :], PT[:, n % 2, c, :],
                                    start=True, stop=True, tile_position=(0, 32 * c))
                fill(PV)(ins)
                for c in range(NC):
                    ins = pe.matmul(bank[SU][32 * c:32 * c + 32, :], w("ones_blk"), PT[:, n % 2, c, :],
                                    start=True, stop=True, tile_position=(0, 32 * c))
                fill(SU)(ins)

            def project(layer, b):
                n = nth_att[(layer, b)]
                may_fill(pe, PQ, "O", layer, b)
                is_read(pe, PV, "PV", layer, b)
                pe.wait_ge(pool_const, WO)
                for j in range(TB):
                    ins = pe.matmul(bank[PQ][:, D * j:D * j + D], AT[:, n % 2, 128 * j:128 * j + 128], wo[layer],
                                    start=True, stop=True)
                fill(PQ)(ins)

            def route_logits(b, key, weight, width, ln):
                may_fill(pe, PQ, key, b)
                is_read(pe, TP, "LN", ln, b)
                for j in range(TB):
                    ins = pe.matmul(bank[PQ][:, width * j:width * j + width], XT[:, b, 128 * j:128 * j + 128],
                                    w(weight), start=True, stop=True)
                fill(PQ)(ins)

            def up0(b, i):
                g, (f0, fn) = i // NF, FCH[i % NF]
                k = ST0 + i % 2
                may_fill(pe, k, "UP0", b, i)
                if i == 0:
                    is_read(pe, TP, "LN", 1, b)
                fill(k)(pe.matmul(bank[k][0:fn, :], wup[:, g, f0:f0 + fn], XT[:, b, :], start=True, stop=True))

            def down0(j, b):
                t = TB * b + j
                if j == 0:
                    is_read(pe, ST0, "UP0", b, NG * NF - 2)
                    is_read(pe, ST1, "UP0", b, NG * NF - 1)
                for g in range(NG):
                    k = DOWN_BANKS[t % 2][g // 2]
                    if g % 2 == 0:
                        may_fill(pe, k, "DN", t)
                    for f, (f0, fn) in enumerate(FCH):
                        ins = pe.matmul(bank[k][:, 2 * D * (g % 2):2 * D * (g % 2) + 2 * D],
                                        MID[0:fn, NF * g + f, b % AHEAD, 128 * j:128 * j + 128],
                                        wdn[0:fn, f, 2 * g:2 * g + 2, :].rearrange("p e h -> p (e h)"),
                                        start=(f == 0), stop=(f == NF - 1))
                    if g % 2 == 1:
                        fill(k)(ins)
                may_fill(pe, PQ, "BD", t)
                fill(PQ)(pe.matmul(bank[PQ][:, 0:D], GT[:], bdn_t[:, t, :], start=True, stop=True))

            def turn_gates(b):
                may_fill(pe, TP, "R1", b)
                pe.wait_ge(g3_done, b + 1)
                o = bank[TP][:].bitcast(BF16)
                for j in range(TB):
                    ins = pe.transpose(o[0:3 * R1, 128 * j:128 * j + 128],
                                       g3[:, j, :, :].rearrange("p a r -> p (a r)"), ident_b[:])
                fill(TP)(ins)

            def up1(b):
                is_read(pe, TP, "LN", 3, b)
                for c in range(CH1):
                    k = ST0 + c % 2
                    may_fill(pe, k, "UP1", b, c)
                    fill(k)(pe.matmul(bank[k][:], wup1[:, 128 * c:128 * c + 128], XT[:, b, :], start=True, stop=True))
                    if c == 1:
                        turn_gates(b)
                    if c >= 2:
                        spread_gate(b, c - 2)
                spread_gate(b, CH1 - 2)

            def spread_gate(b, c):
                k = SM0 + c % 2
                may_fill(pe, k, "GATE", b, c)
                is_read(pe, TP, "R1", b)
                fill(k)(pe.matmul(bank[k][:], gate_rows[0:3 * R1, 2 * c:2 * c + 2, :].rearrange("p r e -> p (r e)"),
                                  gT[0:3 * R1, :], start=True, stop=True))

            def down1(b):
                may_fill(pe, PV, "DN1", b)
                is_read(pe, SM0, "GATE", b, CH1 - 3)
                is_read(pe, SM1, "GATE", b, CH1 - 2)
                is_read(pe, ST0 + (CH1 - 1) % 2, "UP1", b, CH1 - 1)
                for j in range(TB):
                    for c in range(CH1):
                        ins = pe.matmul(bank[PV][:, D * j:D * j + D], HG[:, c, 128 * j:128 * j + 128], wdn1[:, c, :],
                                        start=(c == 0), stop=(c == CH1 - 1))
                fill(PV)(ins)

            pe.wait_ge(w_in, 16)
            keys_values(0)
            turn(0, 0)
            keys_values(1)
            for name, a, b in first:
                if name == "LN" and (a, b) != (0, 0):
                    turn(a, b)
                elif name == "Q":
                    queries(a, b)
                elif name == "SM":
                    scores_for_max(a, b)
                elif name == "NT":
                    turn_max(a, b)
                elif name == "ST":
                    scores(a, b)
                elif name == "PV":
                    attend(a, b)
                elif name == "O":
                    project(a, b)
                elif name == "R0":
                    route_logits(b, "R0", "wr0", E0, 1)
            pe.wait_ge(up_in, 32)
            pieces = [(b, i) for b in range(AHEAD) for i in range(NG * NF)]
            up0(*pieces[0])
            up0(*pieces[1])
            may_fill(pe, TP, "P")
            pe.wait_ge(prob_done, 1)
            fill(TP)(pe.transpose(bank[TP][:, 0:128], P0[:].rearrange("p t e -> p (t e)"), ident))
            del pieces[0:2]
            for i in range(BITS + 1):
                if pieces:
                    up0(*pieces.pop(0))
                may_fill(pe, PQ, "COUNT", i)
                pe.wait_ge(count_done, i + 1)
                if i < BITS:
                    fill(PQ)(pe.matmul(bank[PQ][:, 0:1], same_b[:], count[:, 0:1], start=True, stop=True))
                else:
                    pe.matmul(bank[PQ][:, 0:1], same_b[:], count[:, 0:1], start=True, stop=True)
                    fill(PQ)(pe.matmul(bank[PQ][:, 1:2], before_b[:], count[:, 1:2], start=True, stop=True))
            assert not pieces
            may_fill(pe, TP, "G")
            pe.wait_ge(gt_done, 1)
            fill(TP)(pe.transpose(bank[TP][:, 0:128], GT[:], ident))
            pe.wait_ge(dn_in, 16 * (1 + NF))
            pe.wait_ge(bdn_done, 1)
            for name, a, b in second:
                if name == "LN":
                    turn(a, b)
                elif name == "Q":
                    queries(a, b)
                elif name == "SM":
                    scores_for_max(a, b)
                elif name == "NT":
                    turn_max(a, b)
                elif name == "ST":
                    scores(a, b)
                elif name == "PV":
                    attend(a, b)
                elif name == "O":
                    project(a, b)
                elif name == "DN":
                    down0(a, b)
                elif name == "UP0":
                    for i in range(NG * NF):
                        up0(b, i)
                elif name == "R1":
                    route_logits(b, "R1", "wr1", R1, 3)
                elif name == "UP1":
                    if b == 0:
                        pe.wait_ge(up1_in, 32)
                        pe.wait_ge(pool_const, WDN1)
                    up1(b)
                elif name == "DN1":
                    down1(b)

        @block.vector
        def _(dve):
            links = [0]

            def link(ins):
                links[0] += 1
                ins.then_inc(vec_chain, 1)
                dve.wait_ge(vec_chain, links[0])

            def statistics(a, b):
                t0 = TB * b
                if (a, b) in ((0, 0), (0, 1), (0, 2), (0, 3)):
                    dve.wait_ge(x_in[b], 16)
                elif a == 1:
                    is_read(dve, PQ, "O", 0, b)
                elif a == 2:
                    is_read(dve, PQ, "BD", t0 + TB - 1)
                elif a == 3:
                    is_read(dve, PQ, "O", 1, b)
                for j in range(TB):
                    ins = dve.bn_stats(stats[:, t0 + j, :], X[:, t0 + j, :])
                link(ins)
                for j in range(TB):
                    ins = dve.bn_aggr(mv[:, t0 + j, :], stats[:, t0 + j, :])
                ins.then_inc(var_done, 1)

            def normalise(a, b):
                n = nth_ln[(a, b)]
                dve.wait_ge(var_done, n + 1)
                dve.wait_ge(rstd_done, n + 1)
                if n >= 2:
                    is_full(dve, TP, "LN", *list(nth_ln)[n - 2])
                for j in range(TB):
                    t = TB * b + j
                    ins = dve.tensor_scalar(XN[:, n % 2, j, :], X[:, t, :], mv[:, t, 0:1], rstd[:, t:t + 1],
                                            ALU.subtract, ALU.mult)
                ins.then_inc(xn_done, 1)

            def queries(layer, b):
                n = nth_att[(layer, b)]
                is_read(dve, PQ, "Q", layer, b)
                dve.tensor_copy(QR[:, n % 2, :], QT[:, n % 2, :]).then_inc(qr_done, 1)

            def maxima(layer, b):
                n, t0 = nth_att[(layer, b)], TB * b
                for j in range(TB):
                    k = SM0 + j % 2
                    is_full(dve, k, "SM", layer, b, j)
                    dve.tensor_reduce(mx[:, t0 + j, :], bank[k][:].rearrange("p (h k) -> p h k", h=H), AX_X, ALU.max)\
                        .then_inc(read_out[k], 1)
                is_read(dve, SM0, "SM", layer, b, TB - 2)
                is_read(dve, SM1, "SM", layer, b, TB - 1)
                m = mx[:, t0:t0 + TB, :]
                link(dve.tensor_scalar(nm[:, n % 2, :, 0, :], m, -1.0, None, ALU.mult))
                dve.scalar_tensor_tensor(nm[:, n % 2, :, 1, :], m, -1.0, nm[:, n % 2, :, 0, :], ALU.mult,
                                         ALU.subtract).then_inc(nm_done, 1)

            def max_to_rows(layer, b):
                is_full(dve, TP, "NT", layer, b)
                dve.tensor_copy(shift[0:2 * H, b, :], bank[TP][:].bitcast(BF16)[0:2 * H, 0:S])\
                    .then_inc(read_out[TP], 1)

            def weigh(layer, b):
                n = nth_att[(layer, b)]
                is_full(dve, PV, "PV", layer, b)
                dve.wait_ge(rs_done, n + 1)
                dve.tensor_tensor(AT[:, n % 2, :], bank[PV][:], rsum[:], ALU.mult).then_inc(read_out[PV], 1)

            def add_attention(layer, b):
                n = nth_att[(layer, b)]
                is_full(dve, PQ, "O", layer, b)
                dve.wait_ge(xb_done, n + 1)
                if layer == 0:
                    for j in range(TB):
                        t = TB * b + j
                        ins = dve.scalar_tensor_tensor(X[:, t, :], bank[PQ][:, D * j:D * j + D], any_keep[:, t:t + 1],
                                                       XB[:, n % 2, j, :], ALU.mult, ALU.add)
                else:
                    ins = dve.tensor_tensor(X[:, TB * b:TB * b + TB, :].rearrange("p t h -> p (t h)"), bank[PQ][:],
                                            XB[:, n % 2, :, :].rearrange("p t h -> p (t h)"), ALU.add)
                ins.then_inc(read_out[PQ], 1)

            def combine(j, b):
                t = TB * b + j
                a = acc[:, t % 2, :]
                for e in range(E0):
                    k = DOWN_BANKS[t % 2][e // 4]
                    if e % 4 == 0:
                        is_full(dve, k, "DN", t)
                    ins = dve.scalar_tensor_tensor(a, bank[k][:, D * (e % 4):D * (e % 4) + D], G0[:, t, e:e + 1],
                                                   X[:, t, :] if e == 0 else a, ALU.mult, ALU.add)
                    if e % 4 == 3:
                        ins.then_inc(read_out[k], 1)
                        is_read(dve, k, "DN", t)
                    else:
                        link(ins)
                is_full(dve, PQ, "BD", t)
                dve.tensor_tensor(X[:, t, :], bank[PQ][:, 0:D], a, ALU.add).then_inc(read_out[PQ], 1)

            def gates1(b):
                is_full(dve, PQ, "R1", b)
                lg = bank[PQ][:, 0:TB * R1].rearrange("p (t r) -> p t r", t=TB)
                link(dve.tensor_reduce(m1[:], lg, AX_X, ALU.max))
                dve.tensor_tensor(lg1[:], lg, spread(m1[:], 2, R1), ALU.subtract).then_inc(read_out[PQ], 1)
                dve.wait_ge(e1_done, b + 1)
                p = p1[:, :, 0:R1]
                link(dve.tensor_reduce(s1[:], p, AX_X, ALU.add))
                link(dve.reciprocal(r1[:], s1[:]))
                link(dve.tensor_tensor(p, p, spread(r1[:], 2, R1), ALU.mult))
                for j in range(TB):
                    ins = dve.max(top8[:, j, :], p1[:, j, 0:R1])
                link(ins)
                link(dve.tensor_copy(take8[:, :, 0:TOP1], top8[:, :, 0:TOP1]))
                for j in range(TB):
                    ins = dve.match_replace(rest[:, j, :], take8[:, j, :], p1[:, j, :], 0.0)
                link(ins)
                link(dve.tensor_tensor(gate[:], p, rest[:, :, 0:R1], ALU.subtract))
                link(dve.tensor_copy(g3[:, :, 0, :], gate[:]))
                link(dve.tensor_tensor(gres[:], gate[:], g3[:, :, 0, :], ALU.subtract))
                link(dve.tensor_copy(g3[:, :, 1, :], gres[:]))
                dve.tensor_tensor(g3[:, :, 2, :], gres[:], g3[:, :, 1, :], ALU.subtract).then_inc(g3_done, 1)

            def gate_hidden(b):
                is_full(dve, TP, "R1", b)
                dve.tensor_copy(gT[0:3 * R1, :], bank[TP][:].bitcast(BF16)[0:3 * R1, 0:S]).then_inc(read_out[TP], 1)
                for c in range(CH1 - 1):
                    k = SM0 + c % 2
                    is_full(dve, k, "GATE", b, c)
                    is_read(dve, ST0 + c % 2, "UP1", b, c)
                    dve.tensor_tensor(HG[:, c, :], bank[k][:], HG[:, c, :], ALU.mult).then_inc(read_out[k], 1)

            def add_experts1(b):
                is_full(dve, PV, "DN1", b)
                t = slice(TB * b, TB * b + TB)
                dve.tensor_tensor(X[:, t, :].rearrange("p t h -> p (t h)"), bank[PV][:],
                                  X[:, t, :].rearrange("p t h -> p (t h)"), ALU.add).then_inc(read_out[PV], 1)

            dve.wait_ge(w_in, 16)
            dve.tensor_copy(ctx4[:].rearrange("p b (a k) -> p b a k", a=HC),
                            spread(w("ctxT").rearrange("p (b k) -> p b k", b=B), 2, HC))
            dve.memset(ones_row[:], 1.0).then_inc(vec_const, 1)
            statistics(0, 0)
            dve.tensor_copy(ident_b[:], ident)
            dve.tensor_copy(same_b[:], w("same_e"))
            dve.tensor_copy(before_b[:], w("before")).then_inc(vec_const, 1)
            is_read(dve, PQ, "K", 0)
            for b in range(B):
                ins = dve.tensor_tensor(KB[:, b, :].rearrange("p (h k) -> p h k", h=H), spread(w("headcol"), 2, SK),
                                        spread(kcol[:, 0, SK * b:SK * b + SK], 1, H), ALU.mult)
            ins.then_inc(kb_done[0], 1)
            normalise(0, 0)
            dve.wait_ge(kb_done[0], 1)
            dve.tensor_copy(KR[:], KB[:]).then_inc(kr_done, 1)
            for layer in range(2):
                is_full(dve, SM0, "V", layer)
                dve.tensor_tensor(VB[:, layer, :, :], bank[SM0][:].rearrange("p (n d) -> p n d", d=32),
                                  spread(w("ones_blk"), 1, B * NC), ALU.mult).then_inc(read_out[SM0], 1)
            dve.wait_ge(keep_in, 16)
            link(dve.tensor_scalar(keep_f[:], keep_i[:], 0.0, None, ALU.not_equal))
            dve.tensor_reduce(any_keep[:], keep_f[:], AX_X, ALU.max).then_inc(vec_const, 1)
            dve.wait_ge(vec_const, 3)

            for name, a, b in first:
                if name == "LN" and (a, b) != (0, 0):
                    statistics(a, b)
                    normalise(a, b)
                elif name == "Q":
                    queries(a, b)
                elif name == "SM":
                    maxima(a, b)
                elif name == "NT":
                    max_to_rows(a, b)
                elif name == "PV":
                    weigh(a, b)
                elif name == "O":
                    add_attention(a, b)
                elif name == "R0":
                    is_full(dve, PQ, "R0", b)
                    dve.tensor_tensor(LG[:, TB * b:TB * b + TB, :],
                                      bank[PQ][:, 0:TB * E0].rearrange("p (t e) -> p t e", t=TB),
                                      spread(rows[:, 2 * D:2 * D + E0], 1, TB), ALU.add).then_inc(read_out[PQ], 1)

            is_read(dve, PQ, "R0", B - 1)
            link(dve.tensor_reduce(lmax[:], LG[:], AX_X, ALU.max))
            dve.tensor_tensor(LG[:], LG[:], spread(lmax[:], 2, E0), ALU.subtract).then_inc(lgs_done, 1)
            dve.wait_ge(e0_done, 1)
            link(dve.tensor_reduce(lsm[:], P0[:], AX_X, ALU.add))
            link(dve.reciprocal(lrc[:], lsm[:]))
            dve.tensor_tensor(P0[:], P0[:], spread(lrc[:], 2, E0), ALU.mult).then_inc(prob_done, 1)
            link(dve.memset(cand[:], 1 << (BITS - 1)))
            is_full(dve, TP, "P")
            dve.tensor_copy(PRT[:], bank[TP][:, 0:128]).then_inc(read_out[TP], 1)
            is_read(dve, TP, "P")
            for i in range(BITS):
                dve.tensor_scalar(gt[:], PRT[:], cand[:].bitcast(F32), None, ALU.is_ge, ALU.add,
                                  accum_out=count[:, 0:1]).then_inc(count_done, 1)
                is_full(dve, PQ, "COUNT", i)
                dve.tensor_scalar(over[:], bank[PQ][:, 0:1], float(TOPK0), float(1 << (BITS - 1 - i)), ALU.is_lt,
                                  ALU.mult).then_inc(read_out[PQ], 1)
                is_read(dve, PQ, "COUNT", i)
                following = 1 << (BITS - 2 - i) if i < BITS - 1 else 0
                link(dve.scalar_tensor_tensor(cand[:], over[:], following, cand[:], ALU.bitwise_or, ALU.bitwise_xor))
            dve.tensor_scalar(gt[:], PRT[:], cand[:].bitcast(F32), None, ALU.is_gt, ALU.add, accum_out=count[:, 0:1])
            link(dve.tensor_scalar(eq[:], PRT[:], cand[:].bitcast(F32), None, ALU.is_equal))
            link(dve.tensor_tensor_scan(run[:], eq[:], eq[:], 0.0, ALU.add, ALU.max))
            dve.tensor_copy(count[:, 1:2], run[:, 127:128]).then_inc(count_done, 1)
            is_full(dve, PQ, "COUNT", BITS)
            link(dve.tensor_scalar(left[:, 0:1], bank[PQ][:, 0:1], -1.0, float(TOPK0), ALU.mult, ALU.add))
            dve.tensor_tensor(left[:, 1:2], left[:, 0:1], bank[PQ][:, 1:2], ALU.subtract).then_inc(read_out[PQ], 1)
            is_read(dve, PQ, "COUNT", BITS)
            link(dve.scalar_tensor_tensor(eq[:], run[:], left[:, 1:2], eq[:], ALU.is_le, ALU.mult))
            link(dve.tensor_tensor(gt[:], gt[:], eq[:], ALU.add))
            dve.tensor_tensor(GT[:], gt[:], PRT[:], ALU.mult).then_inc(gt_done, 1)
            is_full(dve, TP, "G")
            dve.tensor_scalar(G0[:].rearrange("p t e -> p (t e)"), bank[TP][:, 0:128], g_tanh[:, 1:2], None, ALU.mult)\
                .then_inc(read_out[TP], 1)
            is_read(dve, TP, "G")
            dve.wait_ge(kb_done[1], 1)
            dve.tensor_copy(KR[:], KB[:]).then_inc(kr_done, 1)
            dve.wait_ge(pool_const, TAKE)

            for name, a, b in second:
                if name == "LN":
                    statistics(a, b)
                    normalise(a, b)
                elif name == "Q":
                    queries(a, b)
                elif name == "SM":
                    maxima(a, b)
                elif name == "NT":
                    max_to_rows(a, b)
                elif name == "PV":
                    weigh(a, b)
                elif name == "O":
                    add_attention(a, b)
                elif name == "DN":
                    combine(a, b)
                elif name == "R1":
                    gates1(b)
                elif name == "UP1":
                    gate_hidden(b)
                elif name == "DN1":
                    add_experts1(b)


_INS = ["x", "mask_tm", "mask_t", "weights", "gates", "w_up", "b_up", "w_down", "b_down", "w_up1", "w_dn1"]


def kernel(x, ctx_1024, mask_BxSxS2_if1, mask_BxSxS2_ik0, g_xattn, g_ffn, L0_xattn_Wq, L0_xattn_bq, L0_xattn_Wk,
           L0_xattn_bk, L0_xattn_Wv, L0_xattn_bv, L0_xattn_Wo, L0_xattn_bo, L0_ffn_Wr, L0_ffn_br, L0_ffn_W_up,
           L0_ffn_b_up, L0_ffn_W_down, L0_ffn_b_down, L1_xattn_W_kv, L1_xattn_b_kv, L1_xattn_W_q, L1_xattn_b_q,
           L1_xattn_W_o, L1_xattn_b_o, L1_ffn_shared_up, L1_ffn_shared_down, L1_ffn_routed_up, L1_ffn_routed_down,
           L1_ffn_router_w):
    import numpy as np
    import concourse.bacc as bacc
    from concourse.bass_utils import run_bass_kernel_spmd

    def on_rows(v):
        return np.broadcast_to(np.asarray(v).reshape(1, -1), (128, np.asarray(v).size))

    wkv = np.asarray(L1_xattn_W_kv).reshape(D, H, 2, DK)
    bkv = np.asarray(L1_xattn_b_kv).reshape(H, 2, DK)
    p, c = np.arange(128)[:, None], np.arange(128)[None, :]
    f32 = np.float32
    parts = {
        "wq0": np.asarray(L0_xattn_Wq).T, "wk0": np.asarray(L0_xattn_Wk).T, "wv0": np.asarray(L0_xattn_Wv).T,
        "wo0": np.asarray(L0_xattn_Wo).T, "ctxT": np.asarray(ctx_1024).reshape(B * SK, D).T,
        "wk1": wkv[:, :, 0].reshape(D, D), "wv1": wkv[:, :, 1].reshape(D, D), "wq1": np.asarray(L1_xattn_W_q),
        "wo1": np.asarray(L1_xattn_W_o), "wr0": np.asarray(L0_ffn_Wr), "wr1": np.asarray(L1_ffn_router_w).T,
        "cols": np.stack([np.asarray(L0_xattn_bq), np.asarray(L0_xattn_bk), np.asarray(L1_xattn_b_q),
                          bkv[:, 0].reshape(D)], 1),
        "rows": np.concatenate([on_rows(L0_xattn_bo), on_rows(L1_xattn_b_o), on_rows(L0_ffn_br),
                                on_rows(L0_xattn_bv), on_rows(bkv[:, 1].reshape(D))], 1),
        "ident": (p == c).astype(f32),
        "same_e": (p % E0 == c % E0).astype(f32),
        "before": ((p % E0 == c % E0) & (p // E0 < c // E0)).astype(f32),
        "headcol": (p // DK == c[:, :H]).astype(f32),
        "ones_blk": (p // SK == c[:, :HC * DK] // DK).astype(f32),
        "key32": (p - 64 == c[:, :SK]).astype(f32),
        "max16": ((p < 2 * H) & (p % H == c[:, :H])).astype(f32),
        "tile16": (p // E0 == c[:, :NT]).astype(f32),
        "gate16": ((p < 3 * R1) & (p % R1 == c[:, :R1])).astype(f32),
    }
    weights = np.concatenate([parts[n] for n in W_COLS], 1)
    b_up = np.zeros((128, NG, NF), f32)
    for k, (f0, fn) in enumerate(FCH):
        b_up[:fn, :, k] = np.asarray(L0_ffn_b_up)[:, f0:f0 + fn].T
    up1 = np.concatenate([np.asarray(L1_ffn_routed_up).reshape(R1 * EH, D),
                          np.asarray(L1_ffn_shared_up).reshape(-1, D)]).T
    dn1 = np.concatenate([np.asarray(L1_ffn_routed_down).transpose(0, 2, 1).reshape(R1 * EH, D),
                          np.asarray(L1_ffn_shared_down).transpose(0, 2, 1).reshape(-1, D)])
    masks = [np.asarray(m).reshape(B * S, SK) for m in (mask_BxSxS2_if1, mask_BxSxS2_ik0)]
    gx, gf = np.asarray(g_xattn), np.asarray(g_ffn)
    given = {
        "x": np.asarray(x).reshape(B * S, D), "mask_tm": masks[0], "mask_t": np.stack([m.T for m in masks]),
        "weights": weights, "gates": on_rows(np.stack([gx[0], gf[0], gx[1], gf[1]])),
        "w_up": np.asarray(L0_ffn_W_up), "b_up": b_up, "w_down": np.asarray(L0_ffn_W_down),
        "b_down": np.tile(np.asarray(L0_ffn_b_down), (NT, 1)), "w_up1": up1,
        "w_dn1": dn1.reshape(CH1, 128, D).transpose(1, 0, 2),
    }
    nc = bacc.Bacc("TRN2", target_bir_lowering=False, num_devices=1)
    arrays, args = {}, []
    for name in _INS:
        a = np.ascontiguousarray(given[name])
        arrays[f"in_{name}"] = a
        args.append(nc.dram_tensor(f"in_{name}", a.shape, mybir.dt.from_np(a.dtype), kind="ExternalInput").ap())
    args.append(nc.dram_tensor("out_x", (B * S, D), F32, kind="ExternalOutput").ap())
    build(nc, *args)
    r = run_bass_kernel_spmd(nc, [arrays], core_ids=[0])
    return r.results[0]["out_x"].reshape(B, S, D)
```

```python
from contextlib import ExitStack

import concourse.bass as bass
from concourse import mybir
from concourse.alu_op_type import AluOpType as ALU

ACT = mybir.ActivationFunctionType
F32 = mybir.dt.float32
F32R = mybir.dt.float32r
BF16 = mybir.dt.bfloat16
I32 = mybir.dt.int32
AX_X = mybir.AxisListType.X

B, S, D, SK, H = 4, 512, 128, 32, 16
DK = D // H
TB = S // 128
NT = B * TB
HC = 4
NC = H // HC
E0, NG, FF = 8, 4, 341
TOPK0 = B * S // E0
FCH = [(0, 128), (128, 128), (256, FF - 256)]
NF = len(FCH)
R1, EH, TOP1 = 16, 64, 4
CH1 = R1 * EH // 128 + 1
LN_EPS = 1e-5
MASKED = -float(2 ** 66)
SCALE = float(DK) ** -0.5
BITS = 30
RADIX_BITS = 2
DIGITS = BITS // RADIX_BITS
TRIES = 2 ** RADIX_BITS - 1
AHEAD = 2

W_COLS = {}
_at = 0
for _n, _w in (("ident", 128), ("cols", 4), ("headcol", H), ("ctxT", B * SK), ("wk0", D),
               ("wq0", D), ("wv0", D), ("ones_blk", 32), ("key32", SK), ("max16", H), ("rows", 4 * D + E0),
               ("wo0", D), ("wo1", D), ("wk1", D), ("wv1", D), ("wq1", D), ("wr0", E0), ("wr1", R1),
               ("same_e", 128), ("before", 128), ("gate16", R1), ("tile16", NT)):
    W_COLS[_n] = (_at, _w)
    _at += _w
NW = _at
W_PARTS = [0, W_COLS["wq0"][0], W_COLS["wo0"][0], NW]


TP, PQ, SM0, SM1, ST0, ST1, PV, SU = range(8)
DOWN_BANKS = [(SM0, SM1), (PV, SU)]
DOWN1_BANKS = [PV, SU]


ORDER = """
    LS:0:0 LA:0:0 LS:0:1 LS:0:3 K:0:0 V:0:0 LN:0:0 K:1:0 LS:0:2 Q:0:0 LA:0:1 V:1:0 LN:0:1 SM:0:0 SM:1:0 SM:2:0 SM:3:0
    Q:0:1 NT:0:0 ST:0:0 LA:0:2 SM:0:1 LN:0:2 LA:0:3 SM:1:1 PV:0:0 WG:0:0 SM:2:1 Q:0:2 LN:0:3 SM:3:1 SM:0:2 O:0:0
    NT:0:1 SM:1:2 SM:2:2 ST:0:1 LS:1:0 PV:0:1 LA:1:0 SM:3:2 WG:0:1 LN:1:0 Q:0:3 NT:0:2 ST:0:2 SM:0:3 O:0:1 LS:1:1
    PV:0:2 SM:1:3 WG:0:2 UP0:0:0 SM:2:3 SM:3:3 O:0:2 UP0:1:0 NT:0:3 ST:0:3 PV:0:3 LS:1:2 LA:1:1 UP0:2:0 WG:0:3 R0:0:0
    LA:1:2 UP0:3:0 LN:1:1 O:0:3 LS:1:3 UP0:4:0 UP0:5:0 UP0:6:0 UP0:7:0 UP0:8:0 UP0:9:0 LN:1:2 UP0:10:0 UP0:11:0 LA:1:3
    UP0:0:1 UP0:1:1 LN:1:3 R0:0:2 UP0:2:1 UP0:3:1 R0:0:1 DN:0:0 R0:0:3 DN:1:0 DN:2:0 RP:0:0 UP0:4:1 UP0:5:1 CT:0:0
    UP0:6:1 UP0:7:1 CT:1:0 DN:3:0 UP0:8:1 CT:2:0 UP0:9:1 DN:4:0 CT:3:0 DN:5:0 UP0:10:1 CT:4:0 DN:6:0 CT:5:0 DN:7:0
    CT:6:0 UP0:11:1 CT:7:0 CT:8:0 CT:9:0 CT:10:0 CT:11:0 CT:12:0 CT:13:0 CT:14:0 CT:15:0 GT:0:0 BD:0:0 BD:1:0 DN:8:0
    DN:9:0 DN:10:0 DN:11:0 DN:12:0 DN:13:0 DN:14:0 BD:2:0 DN:15:0 UP0:0:2 UP0:1:2 DN:0:1 BD:3:0 UP0:2:2 LS:2:0 DN:1:1
    UP0:3:2 LA:2:0 UP0:4:2 DN:2:1 UP0:5:2 DN:3:1 DN:4:1 BD:0:1 LN:2:0 UP0:6:2 DN:5:1 DN:6:1 Q:1:0 UP0:7:2 DN:7:1
    SM:4:0 UP0:8:2 SM:5:0 UP0:9:2 SM:6:0 UP0:10:2 SM:7:0 DN:8:1 UP0:11:2 NT:1:0 BD:1:1 ST:1:0 DN:9:1 PV:1:0 WG:1:0
    DN:10:1 DN:11:1 DN:12:1 BD:2:1 DN:13:1 DN:14:1 DN:15:1 UP0:0:3 O:1:0 UP0:1:3 DN:0:2 DN:1:2 UP0:2:3 LS:3:0 BD:3:1
    LA:3:0 UP0:3:3 LS:2:1 DN:2:2 UP0:4:3 DN:3:2 LN:3:0 UP0:5:3 LA:2:1 DN:4:2 DN:5:2 LN:2:1 UP0:6:3 UP0:7:3 BD:0:2
    UP0:8:3 Q:1:1 DN:6:2 UP1:0:0 UP0:9:3 SM:4:1 R1:1:0 SM:5:1 DN:7:2 SM:6:1 UP0:10:3 SM:7:1 BD:1:2 DN:8:2 DN:9:2
    NT:1:1 UP1:1:0 DN:10:2 ST:1:1 DN:11:2 GA:1:0 TG:1:0 BD:2:2 PV:1:1 SG:0:0 WG:1:1 SG:1:0 UP1:2:0 SG:2:0 DN:12:2
    UP0:11:3 SG:3:0 O:1:1 SG:4:0 DN:13:2 SG:5:0 DN:14:2 SG:6:0 LS:3:1 SG:7:0 DN:15:2 BD:3:2 DN:0:3 DN:1:3 LS:2:2
    DN:2:3 DN1:0:0 DN:3:3 LA:3:1 DN1:1:0 LN:3:1 LA:2:2 BD:0:3 DN1:2:0 R1:1:1 LN:2:2 DN1:3:0 DN:4:3 DN:5:3 GA:1:1 Q:1:2
    DN:6:3 UP1:0:1 SM:4:2 SM:5:2 TG:1:1 SM:6:2 DN:7:3 SM:7:2 DN:8:3 DN:9:3 BD:1:3 NT:1:2 DN:10:3 DN:11:3 BD:2:3 ST:1:2
    SG:0:1 PV:1:2 SG:1:1 WG:1:2 SG:2:1 UP1:1:1 DN:12:3 SG:3:1 DN:13:3 SG:4:1 DN:14:3 SG:5:1 DN:15:3 BD:3:3 LS:2:3
    UP1:2:1 SG:6:1 SG:7:1 O:1:2 LA:2:3 DN1:0:1 LS:3:2 DN1:1:1 LN:2:3 LA:3:2 DN1:2:1 Q:1:3 DN1:3:1 LN:3:2 SM:4:3 SM:5:3
    R1:1:2 GA:1:2 SM:6:3 SM:7:3 UP1:0:2 TG:1:2 UP1:1:2 NT:1:3 SG:0:2 SG:1:2 ST:1:3 SG:2:2 PV:1:3 SG:3:2 WG:1:3 SG:4:2
    SG:5:2 O:1:3 UP1:2:2 LS:3:3 SG:6:2 SG:7:2 DN1:0:2 LA:3:3 DN1:1:2 LN:3:3 DN1:2:2 R1:1:3 GA:1:3 DN1:3:2 UP1:0:3
    TG:1:3 UP1:1:3 SG:0:3 SG:1:3 SG:2:3 UP1:2:3 SG:3:3 SG:4:3 SG:5:3 SG:6:3 SG:7:3 DN1:0:3 DN1:1:3 DN1:2:3 DN1:3:3
"""


def schedule():
    return [(name, int(a), int(b)) for name, a, b in (stage.split(":") for stage in ORDER.split())]


def bank_uses(stages):
    uses = {k: {} for k in range(8)}

    def use(k, *key):
        uses[k][key] = len(uses[k])

    for name, a, b in stages:
        if name == "LN":
            use(TP, name, a, b)
        elif name == "K":
            use(PQ, name, a)
        elif name == "V":
            use(PV, name, a)
        elif name in ("Q", "O"):
            use(PQ, name, a, b)
        elif name == "R0":
            use(PQ, name, b)
        elif name == "SM":
            use(SM0 + a % TB % 2, name, a // TB, b, a % TB)
        elif name == "NT":
            use(TP, name, a, b)
        elif name == "ST":
            for c in range(NC):
                use(ST0 + c % 2, name, a, b, c)
        elif name == "PV":
            use(PV, name, a, b)
            use(SU, name, a, b)
        elif name == "RP":
            use(TP, "P")
        elif name == "CT":
            use(PQ, "COUNT", a)
        elif name == "GT":
            use(TP, "G")
        elif name == "UP0":
            use(ST0 + a % 2, "UP0", b, a)
        elif name == "DN":
            t = TB * b + a // NG
            if a % 2 == 0:
                use(DOWN_BANKS[t % 2][a % NG // 2], "DN", t)
        elif name == "BD":
            use(PQ, "BD", TB * b + a)
        elif name == "R1":
            use(PQ, name, b)
        elif name == "TG":
            use(TP, name, b)
        elif name == "UP1":
            for c in thirds(a):
                use(ST0 + c % 2, name, b, c)
        elif name == "SG":
            use(SM0 + a % 2, "GATE", b, a)
        elif name == "DN1":
            use(DOWN1_BANKS[a % 2], name, b, a)
    return uses


def thirds(part):
    return range(CH1 // 3 * part, CH1 // 3 * part + CH1 // 3)


def spread(ap, axis, n):
    ap = ap.unsqueeze(axis)
    shape = list(ap.shape)
    shape[axis] = n
    return ap.broadcast_to(shape)


def build(nc, x, mask_tm, mask_t, weights, tries_of, gates, w_up, b_up, w_down, b_down, w_up1, w_dn1, out):
    order = schedule()
    uses = bank_uses(order)
    nth_ln = {(a, b): n for n, (a, b) in enumerate([(a, b) for name, a, b in order if name == "LA"])}
    nth_var = {(a, b): n for n, (a, b) in enumerate([(a, b) for name, a, b in order if name == "LS"])}
    nth_att = {(a, b): n for n, (a, b) in enumerate([(a, b) for name, a, b in order if name == "Q"])}
    att = list(nth_att)

    with ExitStack() as ctx:
        def sb(name, shape, dt=F32):
            return ctx.enter_context(nc.sbuf_tensor(name, shape, dt))

        def sem(name):
            return ctx.enter_context(nc.semaphore(name))

        bank = [ctx.enter_context(nc.psum_tensor(f"bank{i}", [128, 512], F32)) for i in range(8)]

        W = sb("W", [128, NW])
        g_raw, g_tanh = sb("g_raw", [128, 4]), sb("g_tanh", [128, 4])
        wup, bup = sb("wup", [128, NG, FF]), sb("bup", [128, NG, NF])
        wdn = sb("wdn", [128, NF, E0, D])
        bdn, bdn_t = sb("bdn", [128, D]), sb("bdn_t", [128, NT, D])
        wup1, wdn1 = sb("wup1", [128, CH1 * 128]), sb("wdn1", [128, CH1, D])
        bk_s = sb("bk_s", [128, 2])
        ident_b = sb("ident_b", [128, 128], BF16)
        same_b, before_b = sb("same_b", [128, 128], BF16), sb("before_b", [128, 128], BF16)
        mask_rows, max_rows = sb("mask_rows", [128, H, SK], BF16), sb("max_rows", [128, H, SK], BF16)
        gate_rows = sb("gate_rows", [128, R1, EH], BF16)
        ctx4, ones_row = sb("ctx4", [128, B, 128]), sb("ones_row", [1, 128])
        any_keep = sb("any_keep", [128, NT])
        X, XB = sb("X", [128, NT, D]), sb("XB", [128, 2, TB, D])
        XN, XT = sb("XN", [128, 2, TB, D]), sb("XT", [128, B, S])
        stats, mv = sb("stats", [128, NT, 6]), sb("mv", [128, NT, 2])
        vare, rstd, minus_half = sb("vare", [128, NT]), sb("rstd", [128, NT]), sb("minus_half", [128, TB])
        QT, QR = sb("QT", [128, 2, S]), sb("QR", [128, 2, S], F32R)
        kcol = sb("kcol", [128, 2, B * SK])
        KB, KR = sb("KB", [128, B, H * SK]), sb("KR", [128, B, H * SK], F32R)
        VB = sb("VB", [128, 2, B * NC, 32])
        shift = sb("shift", [128, B, S], BF16)
        mx, nm = sb("mx", [128, NT, H]), sb("nm", [128, 2, TB, 2, H], BF16)
        PT = sb("PT", [128, 2, NC, S])
        rsum, AT = sb("rsum", [128, S]), sb("AT", [128, 2, S])
        LG, P0 = sb("LG", [128, NT, E0]), sb("P0", [128, NT, E0])
        lmax, lsm, lrc = sb("lmax", [128, NT]), sb("lsm", [128, NT]), sb("lrc", [128, NT])
        PRT, GT = sb("PRT", [128, 128]), sb("GT", [128, 128])
        eq, run, gt = (sb(n, [128, 128]) for n in ("eq", "run", "gt"))
        count, left = sb("count", [128, TRIES], BF16), sb("left", [128, 2])
        tries, reached = sb("tries", [128, DIGITS, TRIES], I32), sb("reached", [128, TRIES])
        cand, digit = sb("cand", [128, 1], I32), sb("digit", [128, 2], I32)
        G0 = sb("G0", [128, NT, E0])
        MID = sb("MID", [128, NG * NF, AHEAD, S])
        acc = sb("acc", [128, 2, D])
        lg1, p1 = sb("lg1", [128, TB, R1]), sb("p1", [128, TB, R1 + 4])
        m1, s1, r1 = sb("m1", [128, TB]), sb("s1", [128, TB]), sb("r1", [128, TB])
        top8, take8 = sb("top8", [128, TB, 8]), sb("take8", [128, TB, 8])
        rest, gate = sb("rest", [128, TB, R1 + 4]), sb("gate", [128, TB, R1])
        gres, g3 = sb("gres", [128, TB, R1]), sb("g3", [128, TB, 3, R1], BF16)
        gT = sb("gT", [128, S], BF16)
        HG = sb("HG", [128, CH1, S])
        mask_i = HG[:, 0:B, :].rearrange("p b s -> p (b s)").bitcast(I32)
        keep_i = HG[:, B, :].rearrange("p (t k) -> p t k", t=NT).bitcast(I32)
        keep_f = HG[:, B + 1, :].rearrange("p (t k) -> p t k", t=NT)

        def w(name):
            at, n = W_COLS[name]
            return W[:, at:at + n]

        cols, rows, ident = w("cols"), w("rows"), w("ident")
        wo = [w("wo0"), w("wo1")]
        bo_g = [rows[:, D * layer:D * layer + D] for layer in range(2)]
        bv = [rows[0:1, 2 * D + E0 + D * layer:3 * D + E0 + D * layer] for layer in range(2)]
        x_dram = x.rearrange("(t p) h -> p t h", p=128)
        out_dram = out.rearrange("(t p) h -> p t h", p=128)

        filled = [sem(f"bank{i}_filled") for i in range(8)]
        read_out = [sem(f"bank{i}_read_out") for i in range(8)]

        def may_fill(eng, k, *key):
            if uses[k][key] > 0:
                eng.wait_ge(read_out[k], uses[k][key])

        def is_full(eng, k, *key):
            eng.wait_ge(filled[k], uses[k][key] + 1)

        def is_read(eng, k, *key):
            eng.wait_ge(read_out[k], uses[k][key] + 1)

        x_in = [sem(f"x_in{b}") for b in range(B)]
        tries_in, g_in, keep_in, up_in, up1_in = (sem(n) for n in ("tries_in", "g_in", "keep_in", "up_in", "up1_in"))
        w_in = [sem(f"w_in{n}") for n in range(3)]
        mask_in = [sem("mask_in0"), sem("mask_in1")]
        dn_in = sem("dn_in")
        tanh_done, mask_done = sem("tanh_done"), [sem("mask_done0"), sem("mask_done1")]
        pool_const, pool_chain, vec_const = sem("pool_const"), sem("pool_chain"), sem("vec_const")
        var_done, rstd_done, xn_done = sem("var_done"), sem("rstd_done"), sem("xn_done")
        kb_done = [sem("kb_done0"), sem("kb_done1")]
        kr_done = sem("kr_done")
        qr_done, nm_done = sem("qr_done"), sem("nm_done")
        rs_done, xb_done = sem("rs_done"), sem("xb_done")
        vec_chain = sem("vec_chain")
        lgs_done, e0_done, count_done = sem("lgs_done"), sem("e0_done"), sem("count_done")
        prob_done, gt_done, bdn_done = sem("prob_done"), sem("gt_done"), sem("bdn_done")
        e1_done, g3_done, experts0_done = sem("e1_done"), sem("g3_done"), sem("experts0_done")
        y_out = sem("y_out")

        HALF, BK, MASK_ROWS, MAX_ROWS, WO, BO, GATE_ROWS, WDN1, TAKE = range(1, 10)

        block = ctx.enter_context(nc.Block())

        @block.sync
        def _(sp):
            for n in range(3):
                part = slice(W_PARTS[n], W_PARTS[n + 1])
                sp.dma_start(W[:, part], weights[:, part]).then_inc(w_in[n], 16)
            sp.dma_start(mask_i[64:96, :], mask_t[0]).then_inc(mask_in[0], 16)
            for b in range(1, B):
                t = slice(TB * b, TB * b + TB)
                sp.dma_start(X[:, t, :], x_dram[:, t, :]).then_inc(x_in[b], 16)
            sp.dma_start(keep_i[:], mask_tm.rearrange("(t p) k -> p t k", p=128)).then_inc(keep_in, 16)
            sp.dma_start(tries[:], tries_of).then_inc(tries_in, 16)
            sp.dma_start(wup[:], w_up.rearrange("g h f -> h g f")).then_inc(up_in, 16)
            sp.dma_start(bup[:], b_up).then_inc(up_in, 16)
            sp.dma_start(bdn[:], b_down).then_inc(dn_in, 16)
            for k, (f0, fn) in enumerate(FCH):
                sp.dma_start(wdn[0:fn, k, :, :], w_down[:, f0:f0 + fn, :].rearrange("e f h -> f e h"))\
                    .then_inc(dn_in, 16)
            sp.dma_start(wup1[:], w_up1).then_inc(up1_in, 16)
            sp.dma_start(wdn1[:], w_dn1).then_inc(up1_in, 16)
            sp.wait_ge(mask_done[0], B)
            sp.dma_start(mask_i[64:96, :], mask_t[1]).then_inc(mask_in[1], 16)
            for b in range(B):
                for j in range(0, TB, 2):
                    is_read(sp, DOWN1_BANKS[0], "DN1", b, j)
                    is_read(sp, DOWN1_BANKS[1], "DN1", b, j + 1)
                    t = slice(TB * b + j, TB * b + j + 2)
                    sp.dma_start(out_dram[:, t, :], X[:, t, :]).then_inc(y_out, 16)
            sp.wait_ge(y_out, 16 * B * TB // 2)

        @block.gpsimd
        def _(pool):
            links = [0]

            def link(ins):
                links[0] += 1
                ins.then_inc(pool_chain, 1)
                pool.wait_ge(pool_chain, links[0])

            def rstd_of(a, b):
                t = slice(TB * b, TB * b + TB)
                pool.wait_ge(var_done, nth_var[(a, b)] + 1)
                link(pool.tensor_scalar(vare[:, t], mv[:, t, 1], LN_EPS, None, ALU.add))
                pool.tensor_tensor(rstd[:, t], vare[:, t], minus_half[:], ALU.pow).then_inc(rstd_done, 1)

            def x_plus_bias(layer, b):
                if layer == 0:
                    pool.wait_ge(x_in[b], 16)
                else:
                    pool.wait_ge(experts0_done, TB * b + TB)
                n = nth_att[(layer, b)]
                if n >= 2:
                    is_read(pool, PQ, "O", *att[n - 2])
                pool.tensor_tensor(XB[:, n % 2, :, :], X[:, TB * b:TB * b + TB, :], spread(bo_g[layer], 1, TB),
                                   ALU.add).then_inc(xb_done, 1)

            def operands_of_layer_1():
                is_read(pool, PQ, "K", 1)
                is_read(pool, ST1, "ST", 0, B - 1, NC - 1)
                for b in range(B):
                    ins = pool.tensor_tensor(KB[:, b, :].rearrange("p (h k) -> p h k", h=H),
                                             spread(w("headcol"), 2, SK),
                                             spread(kcol[:, 1, SK * b:SK * b + SK], 1, H), ALU.mult)
                ins.then_inc(kb_done[1], 1)
                pool.wait_ge(dn_in, 16 * (1 + NF))
                link(pool.tensor_scalar(bdn[:], bdn[:], g_tanh[:, 1:2], None, ALU.mult))
                pool.tensor_tensor(bdn_t[:], spread(bdn[:], 1, NT), spread(w("tile16"), 2, D), ALU.mult)\
                    .then_inc(bdn_done, 1)
                pool.wait_ge(bdn_done, 1)
                pool.tensor_copy(gate_rows[:], spread(w("gate16"), 2, EH)).then_inc(pool_const, 1)
                pool.wait_ge(up1_in, 32)
                pool.tensor_scalar(wdn1[:].rearrange("p c h -> p (c h)"), wdn1[:].rearrange("p c h -> p (c h)"),
                                   g_tanh[:, 3:4], None, ALU.mult).then_inc(pool_const, 1)
                pool.memset(take8[:], -1.0)
                pool.memset(p1[:], -1.0).then_inc(pool_const, 1)

            pool.memset(minus_half[:], -0.5).then_inc(pool_const, 1)
            pool.wait_ge(w_in[0], 16)
            pool.tensor_scalar(bk_s[:], cols[:, 1:4:2], SCALE, None, ALU.mult).then_inc(pool_const, 1)
            rstd_of(0, 0)
            pool.wait_ge(w_in[1], 16)
            pool.tensor_copy(mask_rows[:], spread(w("key32"), 1, H)).then_inc(pool_const, 1)
            pool.tensor_copy(max_rows[:], spread(w("max16"), 2, SK)).then_inc(pool_const, 1)
            rstd_of(0, 1)
            pool.wait_ge(tanh_done, 1)
            pool.wait_ge(w_in[2], 16)
            pool.tensor_scalar(wo[0], wo[0], g_tanh[:, 0:1], None, ALU.mult)
            pool.tensor_scalar(wo[1], wo[1], g_tanh[:, 2:3], None, ALU.mult).then_inc(pool_const, 1)
            pool.tensor_scalar(bo_g[0], bo_g[0], g_tanh[:, 0:1], None, ALU.mult)
            pool.tensor_scalar(bo_g[1], bo_g[1], g_tanh[:, 2:3], None, ALU.mult).then_inc(pool_const, 1)
            pool.wait_ge(pool_const, BO)

            for name, a, b in order:
                if name == "LS" and (a, b) not in ((0, 0), (0, 1)):
                    rstd_of(a, b)
                if name == "Q" and a == 0:
                    x_plus_bias(0, b)
                if name == "LS" and a == 2:
                    x_plus_bias(1, b)
                if name == "RP":
                    operands_of_layer_1()

        @block.scalar
        def _(act):
            act.dma_start(X[:, 0:TB, :], x_dram[:, 0:TB, :]).then_inc(x_in[0], 16)
            act.dma_start(g_raw[:], gates).then_inc(g_in, 16)
            act.preload_act_table_set("exp_and_others")
            act.wait_ge(g_in, 16)
            act.activation(g_tanh[:], g_raw[:], ACT.Tanh).then_inc(tanh_done, 1)
            act.preload_act_table_set("natural_log_exp_and_others")
            act.wait_ge(pool_const, BK)

            table = ["natural_log_exp_and_others"]

            def tables(name):
                if table[0] != name:
                    act.preload_act_table_set(name)
                    table[0] = name

            def keys(layer):
                is_full(act, PQ, "K", layer)
                act.activation(kcol[:, layer, :], bank[PQ][:, 0:B * SK], ACT.Identity, bias=bk_s[:, layer:layer + 1],
                               scale=SCALE).then_inc(read_out[PQ], 1)

            def normalised(a, b):
                is_full(act, TP, "LN", a, b)
                act.activation(XT[:, b, :], bank[TP][:], ACT.Copy).then_inc(read_out[TP], 1)

            def queries(layer, b):
                is_full(act, PQ, "Q", layer, b)
                act.activation(QT[:, nth_att[(layer, b)] % 2, :], bank[PQ][:], ACT.Identity,
                               bias=cols[:, 2 * layer:2 * layer + 1]).then_inc(read_out[PQ], 1)

            def exps(layer, b):
                n = nth_att[(layer, b)]
                tables("natural_log_exp_and_others")
                if n >= 2:
                    is_full(act, SU, "PV", *att[n - 2])
                for c in range(NC):
                    k = ST0 + c % 2
                    is_full(act, k, "ST", layer, b, c)
                    act.activation(PT[:, n % 2, c, :], bank[k][:], ACT.Exp).then_inc(read_out[k], 1)

            def inverse_sums(layer, b):
                n = nth_att[(layer, b)]
                tables("natural_log_exp_and_others")
                is_full(act, SU, "PV", layer, b)
                if n >= 1:
                    is_read(act, PV, "PV", *att[n - 1])
                act.activation(rsum[:], bank[SU][:], ACT.Ln).then_inc(read_out[SU], 1)
                is_read(act, SU, "PV", layer, b)
                act.activation(rsum[:], rsum[:], ACT.Exp, scale=-1.0).then_inc(rs_done, 1)

            def hidden0(b, i):
                g, (f0, fn) = i // NF, FCH[i % NF]
                tables("silu_and_others")
                if b >= AHEAD and i == 0:
                    is_full(act, DOWN_BANKS[1][1], "DN", TB * (b - AHEAD) + TB - 1)
                k = ST0 + i % 2
                is_full(act, k, "UP0", b, i)
                act.activation(MID[0:fn, i, b % AHEAD, :], bank[k][0:fn, :], ACT.Silu,
                               bias=bup[0:fn, g, i % NF:i % NF + 1]).then_inc(read_out[k], 1)

            for name, a, b in order:
                if name == "K":
                    keys(a)
                elif name == "LN":
                    normalised(a, b)
                elif name == "Q":
                    queries(a, b)
                elif name == "ST":
                    exps(a, b)
                elif name == "PV":
                    inverse_sums(a, b)
                elif name == "RP":
                    tables("natural_log_exp_and_others")
                    act.wait_ge(lgs_done, 1)
                    act.activation(P0[:].rearrange("p t e -> p (t e)"), LG[:].rearrange("p t e -> p (t e)"), ACT.Exp)\
                        .then_inc(e0_done, 1)
                elif name == "UP0":
                    if (a, b) == (0, 0):
                        act.wait_ge(up_in, 32)
                    hidden0(b, a)
                elif name == "R1":
                    tables("natural_log_exp_and_others")
                    is_read(act, PQ, "R1", b)
                    act.activation(p1[:, :, 0:R1], lg1[:], ACT.Exp).then_inc(e1_done, 1)
                elif name == "UP1":
                    tables("gelu_and_others")
                    for c in thirds(a):
                        k = ST0 + c % 2
                        is_full(act, k, "UP1", b, c)
                        if b == 0 and c == 0:
                            act.wait_ge(mask_done[1], 1)
                        if b >= 1 and c == 0:
                            is_full(act, DOWN1_BANKS[1], "DN1", b - 1, TB - 1)
                        act.activation(HG[:, c, :], bank[k][:], ACT.Gelu).then_inc(read_out[k], 1)

        @block.tensor
        def _(pe):
            def fill(k):
                return lambda ins: ins.then_inc(filled[k], 1)

            def turn(a, b):
                may_fill(pe, TP, "LN", a, b)
                n = nth_ln[(a, b)]
                for j in range(TB):
                    pe.wait_ge(xn_done, TB * n + j + 1)
                    ins = pe.transpose(bank[TP][:, 128 * j:128 * j + 128], XN[:, n % 2, j, :], ident)
                fill(TP)(ins)

            def keys(layer):
                pe.wait_ge(w_in[2 * layer], 16)
                may_fill(pe, PQ, "K", layer)
                fill(PQ)(pe.matmul(bank[PQ][:, 0:B * SK], w(f"wk{layer}"), w("ctxT"), start=True, stop=True))

            def values(layer):
                pe.wait_ge(w_in[2 * layer], 16)
                may_fill(pe, PV, "V", layer)
                if layer == 0:
                    pe.wait_ge(vec_const, 1)
                    pe.wait_ge(w_in[1], 16)
                for b in range(B):
                    o = bank[PV][:, D * b:D * b + D]
                    pe.matmul(o, ctx4[:, b, :], w(f"wv{layer}"), start=True, stop=False)
                    ins = pe.matmul(o, ones_row[:], bv[layer], start=False, stop=True)
                fill(PV)(ins)

            def queries(layer, b):
                may_fill(pe, PQ, "Q", layer, b)
                if (layer, b) == (0, 0):
                    pe.wait_ge(w_in[1], 16)
                is_read(pe, TP, "LN", 2 * layer, b)
                fill(PQ)(pe.matmul(bank[PQ][:], w(f"wq{layer}"), XT[:, b, :], start=True, stop=True))

            def scores_for_max(part, b):
                layer, j = divmod(part, TB)
                n = nth_att[(layer, b)]
                pe.wait_ge(qr_done, n + 1)
                if j == 0:
                    pe.wait_ge(kr_done, b + 1 if layer == 0 else B + 1)
                    pe.wait_ge(mask_done[layer], b + 1 if layer == 0 else 1)
                    pe.wait_ge(pool_const, MASK_ROWS)
                k = SM0 + j % 2
                may_fill(pe, k, "SM", layer, b, j)
                t = slice(128 * j, 128 * j + 128)
                pe.matmul(bank[k][:], QR[:, n % 2, t], KR[:, b, :], start=True, stop=False)
                fill(k)(pe.matmul(bank[k][:], shift[:, b, t], mask_rows[:].rearrange("p h k -> p (h k)"),
                                  start=False, stop=True))

            def turn_max(layer, b):
                n = nth_att[(layer, b)]
                may_fill(pe, TP, "NT", layer, b)
                pe.wait_ge(nm_done, n + 1)
                pe.wait_ge(vec_const, 2)
                o = bank[TP][:].bitcast(BF16)
                for j in range(TB):
                    ins = pe.transpose(o[0:2 * H, 128 * j:128 * j + 128],
                                       nm[:, n % 2, j, :, :].rearrange("p a h -> p (a h)"), ident_b[:])
                fill(TP)(ins)

            def scores(layer, b):
                n = nth_att[(layer, b)]
                is_read(pe, PQ, "Q", layer, b)
                pe.wait_ge(kb_done[layer], b + 1 if layer == 0 else 1)
                pe.wait_ge(pool_const, MAX_ROWS)
                for c in range(NC):
                    k = ST0 + c % 2
                    may_fill(pe, k, "ST", layer, b, c)
                    r = slice(128 * c, 128 * c + 128)
                    pe.matmul(bank[k][:], KB[:, b, r], QT[:, n % 2, :], start=True, stop=False)
                    if c == 0:
                        is_read(pe, TP, "NT", layer, b)
                    pe.matmul(bank[k][:], mask_rows[:].rearrange("p h k -> p (h k)")[:, r], shift[:, b, :],
                              start=False, stop=False)
                    fill(k)(pe.matmul(bank[k][:], max_rows[:].rearrange("p h k -> p (h k)")[:, r], shift[:, b, :],
                                      start=False, stop=True))

            def attend(layer, b):
                n = nth_att[(layer, b)]
                may_fill(pe, PV, "PV", layer, b)
                may_fill(pe, SU, "PV", layer, b)
                is_read(pe, PV, "V", layer)
                for c in range(NC):
                    is_read(pe, ST0 + c % 2, "ST", layer, b, c)
                    ins = pe.matmul(bank[PV][32 * c:32 * c + 32, :], VB[:, layer, NC * b + c, :], PT[:, n % 2, c, :],
                                    start=True, stop=True, tile_position=(0, 32 * c))
                fill(PV)(ins)
                for c in range(NC):
                    ins = pe.matmul(bank[SU][32 * c:32 * c + 32, :], w("ones_blk"), PT[:, n % 2, c, :],
                                    start=True, stop=True, tile_position=(0, 32 * c))
                fill(SU)(ins)

            def project(layer, b):
                n = nth_att[(layer, b)]
                may_fill(pe, PQ, "O", layer, b)
                is_read(pe, PV, "PV", layer, b)
                pe.wait_ge(pool_const, WO)
                for j in range(TB):
                    ins = pe.matmul(bank[PQ][:, D * j:D * j + D], AT[:, n % 2, 128 * j:128 * j + 128], wo[layer],
                                    start=True, stop=True)
                fill(PQ)(ins)

            def route_logits(b, key, weight, width, ln):
                may_fill(pe, PQ, key, b)
                is_read(pe, TP, "LN", ln, b)
                for j in range(TB):
                    ins = pe.matmul(bank[PQ][:, width * j:width * j + width], XT[:, b, 128 * j:128 * j + 128],
                                    w(weight), start=True, stop=True)
                fill(PQ)(ins)

            def up0(b, i):
                g, (f0, fn) = i // NF, FCH[i % NF]
                k = ST0 + i % 2
                may_fill(pe, k, "UP0", b, i)
                if i == 0:
                    is_read(pe, TP, "LN", 1, b)
                fill(k)(pe.matmul(bank[k][0:fn, :], wup[:, g, f0:f0 + fn], XT[:, b, :], start=True, stop=True))

            def down0(part, b):
                j, g = divmod(part, NG)
                t = TB * b + j
                k = DOWN_BANKS[t % 2][g // 2]
                if g % 2 == 0:
                    may_fill(pe, k, "DN", t)
                for f, (f0, fn) in enumerate(FCH):
                    if j == 0:
                        is_read(pe, ST0 + (NF * g + f) % 2, "UP0", b, NF * g + f)
                    ins = pe.matmul(bank[k][:, 2 * D * (g % 2):2 * D * (g % 2) + 2 * D],
                                    MID[0:fn, NF * g + f, b % AHEAD, 128 * j:128 * j + 128],
                                    wdn[0:fn, f, 2 * g:2 * g + 2, :].rearrange("p e h -> p (e h)"),
                                    start=(f == 0), stop=(f == NF - 1))
                if g % 2 == 1:
                    fill(k)(ins)

            def count_all_tiles(i):
                may_fill(pe, PQ, "COUNT", i)
                pe.wait_ge(count_done, i + 1)
                if i < DIGITS:
                    fill(PQ)(pe.matmul(bank[PQ][:, 0:TRIES], same_b[:], count[:, 0:TRIES], start=True, stop=True))
                else:
                    pe.matmul(bank[PQ][:, 0:1], same_b[:], count[:, 0:1], start=True, stop=True)
                    fill(PQ)(pe.matmul(bank[PQ][:, 1:2], before_b[:], count[:, 1:2], start=True, stop=True))

            def turn_gates(b):
                may_fill(pe, TP, "TG", b)
                pe.wait_ge(g3_done, b + 1)
                o = bank[TP][:].bitcast(BF16)
                for j in range(TB):
                    ins = pe.transpose(o[0:3 * R1, 128 * j:128 * j + 128],
                                       g3[:, j, :, :].rearrange("p a r -> p (a r)"), ident_b[:])
                fill(TP)(ins)

            def up1(part, b):
                is_read(pe, TP, "LN", 3, b)
                for c in thirds(part):
                    k = ST0 + c % 2
                    may_fill(pe, k, "UP1", b, c)
                    fill(k)(pe.matmul(bank[k][:], wup1[:, 128 * c:128 * c + 128], XT[:, b, :], start=True, stop=True))

            def spread_gate(b, c):
                k = SM0 + c % 2
                may_fill(pe, k, "GATE", b, c)
                is_read(pe, TP, "TG", b)
                fill(k)(pe.matmul(bank[k][:], gate_rows[0:3 * R1, 2 * c:2 * c + 2, :].rearrange("p r e -> p (r e)"),
                                  gT[0:3 * R1, :], start=True, stop=True))

            def down1(j, b):
                k = DOWN1_BANKS[j % 2]
                may_fill(pe, k, "DN1", b, j)
                for c in range(CH1):
                    if j == 0 and c < CH1 - 1:
                        is_read(pe, SM0 + c % 2, "GATE", b, c)
                    elif j == 0:
                        is_read(pe, ST0 + c % 2, "UP1", b, c)
                    ins = pe.matmul(bank[k][:, 0:D], HG[:, c, 128 * j:128 * j + 128], wdn1[:, c, :],
                                    start=(c == 0), stop=(c == CH1 - 1))
                fill(k)(ins)

            for name, a, b in order:
                if name == "K":
                    keys(a)
                elif name == "V":
                    values(a)
                elif name == "LN":
                    turn(a, b)
                elif name == "Q":
                    queries(a, b)
                elif name == "SM":
                    scores_for_max(a, b)
                elif name == "NT":
                    turn_max(a, b)
                elif name == "ST":
                    scores(a, b)
                elif name == "PV":
                    attend(a, b)
                elif name == "O":
                    project(a, b)
                elif name == "R0":
                    route_logits(b, "R0", "wr0", E0, 1)
                elif name == "UP0":
                    if (a, b) == (0, 0):
                        pe.wait_ge(up_in, 32)
                    up0(b, a)
                elif name == "RP":
                    may_fill(pe, TP, "P")
                    pe.wait_ge(prob_done, 1)
                    fill(TP)(pe.transpose(bank[TP][:, 0:128], P0[:].rearrange("p t e -> p (t e)"), ident))
                elif name == "CT":
                    count_all_tiles(a)
                elif name == "GT":
                    may_fill(pe, TP, "G")
                    pe.wait_ge(gt_done, 1)
                    fill(TP)(pe.transpose(bank[TP][:, 0:128], GT[:], ident))
                elif name == "DN":
                    if (a, b) == (0, 0):
                        pe.wait_ge(dn_in, 16 * (1 + NF))
                    down0(a, b)
                elif name == "BD":
                    t = TB * b + a
                    may_fill(pe, PQ, "BD", t)
                    pe.wait_ge(gt_done, 1)
                    pe.wait_ge(bdn_done, 1)
                    fill(PQ)(pe.matmul(bank[PQ][:, 0:D], GT[:], bdn_t[:, t, :], start=True, stop=True))
                elif name == "R1":
                    route_logits(b, "R1", "wr1", R1, 3)
                elif name == "UP1":
                    if b == 0 and a == 0:
                        pe.wait_ge(up1_in, 32)
                        pe.wait_ge(pool_const, WDN1)
                    up1(a, b)
                elif name == "TG":
                    turn_gates(b)
                elif name == "SG":
                    spread_gate(b, a)
                elif name == "DN1":
                    down1(a, b)

        @block.vector
        def _(dve):
            links = [0]

            def link(ins):
                links[0] += 1
                ins.then_inc(vec_chain, 1)
                dve.wait_ge(vec_chain, links[0])

            def statistics(a, b):
                t0 = TB * b
                if (a, b) in ((0, 0), (0, 1), (0, 2), (0, 3)):
                    dve.wait_ge(x_in[b], 16)
                elif a == 1:
                    is_read(dve, PQ, "O", 0, b)
                elif a == 2:
                    dve.wait_ge(experts0_done, t0 + TB)
                elif a == 3:
                    is_read(dve, PQ, "O", 1, b)
                for j in range(TB):
                    ins = dve.bn_stats(stats[:, t0 + j, :], X[:, t0 + j, :])
                link(ins)
                for j in range(TB):
                    ins = dve.bn_aggr(mv[:, t0 + j, :], stats[:, t0 + j, :])
                ins.then_inc(var_done, 1)

            def normalise(a, b):
                n = nth_ln[(a, b)]
                dve.wait_ge(var_done, nth_var[(a, b)] + 1)
                dve.wait_ge(rstd_done, nth_var[(a, b)] + 1)
                if n >= 2:
                    is_full(dve, TP, "LN", *list(nth_ln)[n - 2])
                for j in range(TB):
                    t = TB * b + j
                    dve.tensor_scalar(XN[:, n % 2, j, :], X[:, t, :], mv[:, t, 0:1], rstd[:, t:t + 1],
                                      ALU.subtract, ALU.mult).then_inc(xn_done, 1)

            def queries(layer, b):
                n = nth_att[(layer, b)]
                is_read(dve, PQ, "Q", layer, b)
                dve.tensor_copy(QR[:, n % 2, :], QT[:, n % 2, :]).then_inc(qr_done, 1)

            def maxima(part, b):
                layer, j = divmod(part, TB)
                n, t0 = nth_att[(layer, b)], TB * b
                k = SM0 + j % 2
                is_full(dve, k, "SM", layer, b, j)
                dve.tensor_reduce(mx[:, t0 + j, :], bank[k][:].rearrange("p (h k) -> p h k", h=H), AX_X, ALU.max)\
                    .then_inc(read_out[k], 1)
                if j < TB - 1:
                    return
                is_read(dve, SM0, "SM", layer, b, TB - 2)
                is_read(dve, SM1, "SM", layer, b, TB - 1)
                m = mx[:, t0:t0 + TB, :]
                link(dve.tensor_scalar(nm[:, n % 2, :, 0, :], m, -1.0, None, ALU.mult))
                dve.scalar_tensor_tensor(nm[:, n % 2, :, 1, :], m, -1.0, nm[:, n % 2, :, 0, :], ALU.mult,
                                         ALU.subtract).then_inc(nm_done, 1)

            def max_to_rows(layer, b):
                is_full(dve, TP, "NT", layer, b)
                dve.tensor_copy(shift[0:2 * H, b, :], bank[TP][:].bitcast(BF16)[0:2 * H, 0:S])\
                    .then_inc(read_out[TP], 1)

            def weigh(layer, b):
                n = nth_att[(layer, b)]
                is_full(dve, PV, "PV", layer, b)
                dve.wait_ge(rs_done, n + 1)
                dve.tensor_tensor(AT[:, n % 2, :], bank[PV][:], rsum[:], ALU.mult).then_inc(read_out[PV], 1)

            def add_attention(layer, b):
                n = nth_att[(layer, b)]
                is_full(dve, PQ, "O", layer, b)
                dve.wait_ge(xb_done, n + 1)
                if layer == 0:
                    for j in range(TB):
                        t = TB * b + j
                        ins = dve.scalar_tensor_tensor(X[:, t, :], bank[PQ][:, D * j:D * j + D], any_keep[:, t:t + 1],
                                                       XB[:, n % 2, j, :], ALU.mult, ALU.add)
                else:
                    ins = dve.tensor_tensor(X[:, TB * b:TB * b + TB, :].rearrange("p t h -> p (t h)"), bank[PQ][:],
                                            XB[:, n % 2, :, :].rearrange("p t h -> p (t h)"), ALU.add)
                ins.then_inc(read_out[PQ], 1)

            def combine(j, b):
                t = TB * b + j
                banks = DOWN_BANKS[t % 2]
                sums = [acc[:, 0, :], acc[:, 1, :]]
                is_full(dve, PQ, "BD", t)
                dve.tensor_tensor(X[:, t, :], bank[PQ][:, 0:D], X[:, t, :], ALU.add).then_inc(read_out[PQ], 1)
                if t > 0:
                    dve.wait_ge(experts0_done, t)
                done = links[0]
                for e in range(E0 // 2):
                    for half, k in ((1, banks[1]), (0, banks[0])):
                        out, part = sums[half], bank[k][:, D * e:D * e + D]
                        gate = G0[:, t, E0 // 2 * half + e:E0 // 2 * half + e + 1]
                        if e == 0:
                            is_full(dve, k, "DN", t)
                        else:
                            dve.wait_ge(vec_chain, done + 2 * e - half)
                        if e == 0 and half == 1:
                            ins = dve.tensor_scalar(out, part, gate, None, ALU.mult)
                        else:
                            if e == 0:
                                is_read(dve, PQ, "BD", t)
                            ins = dve.scalar_tensor_tensor(out, part, gate, X[:, t, :] if e == 0 else out, ALU.mult,
                                                           ALU.add)
                        ins.then_inc(vec_chain if e < E0 // 2 - 1 else read_out[k], 1)
                links[0] += E0 - 2
                for k in banks:
                    is_read(dve, k, "DN", t)
                dve.tensor_tensor(X[:, t, :], sums[0], sums[1], ALU.add).then_inc(experts0_done, 1)

            def logits1(b):
                is_full(dve, PQ, "R1", b)
                lg = bank[PQ][:, 0:TB * R1].rearrange("p (t r) -> p t r", t=TB)
                link(dve.tensor_reduce(m1[:], lg, AX_X, ALU.max))
                dve.tensor_tensor(lg1[:], lg, spread(m1[:], 2, R1), ALU.subtract).then_inc(read_out[PQ], 1)

            def gates1(b):
                dve.wait_ge(e1_done, b + 1)
                p = p1[:, :, 0:R1]
                link(dve.tensor_reduce(s1[:], p, AX_X, ALU.add))
                link(dve.reciprocal(r1[:], s1[:]))
                link(dve.tensor_tensor(p, p, spread(r1[:], 2, R1), ALU.mult))
                for j in range(TB):
                    ins = dve.max(top8[:, j, :], p1[:, j, 0:R1])
                link(ins)
                link(dve.tensor_copy(take8[:, :, 0:TOP1], top8[:, :, 0:TOP1]))
                for j in range(TB):
                    ins = dve.match_replace(rest[:, j, :], take8[:, j, :], p1[:, j, :], 0.0)
                link(ins)
                link(dve.tensor_tensor(gate[:], p, rest[:, :, 0:R1], ALU.subtract))
                link(dve.tensor_copy(g3[:, :, 0, :], gate[:]))
                link(dve.tensor_tensor(gres[:], gate[:], g3[:, :, 0, :], ALU.subtract))
                link(dve.tensor_copy(g3[:, :, 1, :], gres[:]))
                dve.tensor_tensor(g3[:, :, 2, :], gres[:], g3[:, :, 1, :], ALU.subtract).then_inc(g3_done, 1)

            def gates_to_rows(b):
                is_full(dve, TP, "TG", b)
                dve.tensor_copy(gT[0:3 * R1, :], bank[TP][:].bitcast(BF16)[0:3 * R1, 0:S]).then_inc(read_out[TP], 1)

            def gate_hidden(c, b):
                k = SM0 + c % 2
                is_full(dve, k, "GATE", b, c)
                is_read(dve, ST0 + c % 2, "UP1", b, c)
                dve.tensor_tensor(HG[:, c, :], bank[k][:], HG[:, c, :], ALU.mult).then_inc(read_out[k], 1)

            def add_experts1(j, b):
                k = DOWN1_BANKS[j % 2]
                is_full(dve, k, "DN1", b, j)
                t = TB * b + j
                dve.tensor_tensor(X[:, t, :], bank[k][:, 0:D], X[:, t, :], ALU.add).then_inc(read_out[k], 1)

            def mask_to_rows(layer, batches):
                dve.wait_ge(mask_in[layer], 16)
                if layer == 1:
                    is_read(dve, ST1, "ST", 0, B - 1, NC - 1)
                dve.tensor_scalar(shift[64:96, batches, :], mask_i[64:96, :].rearrange("p (b s) -> p b s", b=B)
                                  [:, batches, :], 0.0, MASKED, ALU.is_equal, ALU.mult).then_inc(mask_done[layer], 1)

            def head_keys(b):
                is_read(dve, PQ, "K", 0)
                dve.tensor_tensor(KB[:, b, :].rearrange("p (h k) -> p h k", h=H), spread(w("headcol"), 2, SK),
                                  spread(kcol[:, 0, SK * b:SK * b + SK], 1, H), ALU.mult).then_inc(kb_done[0], 1)
                dve.wait_ge(kb_done[0], b + 1)
                dve.tensor_copy(KR[:, b, :], KB[:, b, :]).then_inc(kr_done, 1)

            def values(layer):
                is_full(dve, PV, "V", layer)
                dve.tensor_tensor(VB[:, layer, :, :], bank[PV][:].rearrange("p (n d) -> p n d", d=32),
                                  spread(w("ones_blk"), 1, B * NC), ALU.mult).then_inc(read_out[PV], 1)

            def probabilities():
                for b in range(B):
                    is_read(dve, PQ, "R0", b)
                link(dve.tensor_reduce(lmax[:], LG[:], AX_X, ALU.max))
                dve.tensor_tensor(LG[:], LG[:], spread(lmax[:], 2, E0), ALU.subtract).then_inc(lgs_done, 1)
                dve.wait_ge(e0_done, 1)
                link(dve.tensor_reduce(lsm[:], P0[:], AX_X, ALU.add))
                link(dve.reciprocal(lrc[:], lsm[:]))
                dve.tensor_tensor(P0[:], P0[:], spread(lrc[:], 2, E0), ALU.mult).then_inc(prob_done, 1)
                dve.tensor_copy(same_b[:], w("same_e"))
                dve.tensor_copy(before_b[:], w("before"))
                dve.memset(cand[:], 0)
                dve.wait_ge(tries_in, 16)
                is_full(dve, TP, "P")
                dve.tensor_copy(PRT[:], bank[TP][:, 0:128]).then_inc(read_out[TP], 1)
                is_read(dve, TP, "P")

            def one_digit(i):
                for k in range(TRIES):
                    ins = dve.tensor_scalar((gt, eq, run)[k][:], PRT[:], tries[:, i, k:k + 1].bitcast(F32), None, ALU.is_ge,
                                            ALU.add, accum_out=count[:, k:k + 1])
                ins.then_inc(count_done, 1)
                if 0 < i < DIGITS - 1:
                    link(dve.tensor_tensor(tries[:, i + 1, :], tries[:, i + 1, :],
                                           cand[:].broadcast_to([128, TRIES]), ALU.bitwise_or))
                is_full(dve, PQ, "COUNT", i)
                dve.tensor_scalar(reached[:], bank[PQ][:, 0:TRIES], float(TOPK0),
                                  float(1 << (BITS - RADIX_BITS * (i + 1))), ALU.is_ge, ALU.mult)\
                    .then_inc(read_out[PQ], 1)
                is_read(dve, PQ, "COUNT", i)
                d = digit[:, i % 2:i % 2 + 1]
                with nc.allow_low_precision(reason="the sum is a small multiple of a power of two"):
                    link(dve.tensor_reduce(d, reached[:], AX_X, ALU.add))
                if i < DIGITS - 1:
                    link(dve.tensor_tensor(tries[:, i + 1, :], tries[:, i + 1, :], d.broadcast_to([128, TRIES]),
                                           ALU.bitwise_or))
                link(dve.tensor_tensor(cand[:], cand[:], d, ALU.bitwise_or))

            def take():
                dve.tensor_scalar(gt[:], PRT[:], cand[:].bitcast(F32), None, ALU.is_gt, ALU.add, accum_out=count[:, 0:1])
                link(dve.tensor_scalar(eq[:], PRT[:], cand[:].bitcast(F32), None, ALU.is_equal))
                link(dve.tensor_tensor_scan(run[:], eq[:], eq[:], 0.0, ALU.add, ALU.max))
                dve.tensor_copy(count[:, 1:2], run[:, 127:128]).then_inc(count_done, 1)
                is_full(dve, PQ, "COUNT", DIGITS)
                link(dve.tensor_scalar(left[:, 0:1], bank[PQ][:, 0:1], -1.0, float(TOPK0), ALU.mult, ALU.add))
                dve.tensor_tensor(left[:, 1:2], left[:, 0:1], bank[PQ][:, 1:2], ALU.subtract).then_inc(read_out[PQ], 1)
                is_read(dve, PQ, "COUNT", DIGITS)
                link(dve.scalar_tensor_tensor(eq[:], run[:], left[:, 1:2], eq[:], ALU.is_le, ALU.mult))
                link(dve.tensor_tensor(gt[:], gt[:], eq[:], ALU.add))
                dve.tensor_tensor(GT[:], gt[:], PRT[:], ALU.mult).then_inc(gt_done, 1)

            def gates0():
                is_full(dve, TP, "G")
                dve.tensor_scalar(G0[:].rearrange("p t e -> p (t e)"), bank[TP][:, 0:128], g_tanh[:, 1:2], None, ALU.mult)\
                    .then_inc(read_out[TP], 1)
                is_read(dve, TP, "G")
                mask_to_rows(1, slice(0, B))
                dve.wait_ge(kb_done[1], 1)
                dve.tensor_copy(KR[:], KB[:]).then_inc(kr_done, 1)
                dve.wait_ge(pool_const, TAKE)

            link(dve.memset(shift[:], 0.0))
            dve.wait_ge(w_in[0], 16)
            dve.tensor_copy(ctx4[:].rearrange("p b (a k) -> p b a k", a=HC),
                            spread(w("ctxT").rearrange("p (b k) -> p b k", b=B), 2, HC))
            dve.memset(ones_row[:], 1.0).then_inc(vec_const, 1)
            statistics(0, 0)
            dve.tensor_copy(ident_b[:], ident).then_inc(vec_const, 1)
            for name, a, b in order:
                if name == "LS" and (a, b) != (0, 0):
                    statistics(a, b)
                elif name == "LA":
                    if (a, b) == (0, 0):
                        head_keys(b)
                    normalise(a, b)
                    if a == 0:
                        if b > 0:
                            head_keys(b)
                        mask_to_rows(0, slice(b, b + 1))
                elif name == "V":
                    values(a)
                elif name == "Q":
                    queries(a, b)
                elif name == "SM":
                    maxima(a, b)
                elif name == "NT":
                    max_to_rows(a, b)
                    if (a, b) == (0, 0):
                        dve.wait_ge(keep_in, 16)
                        link(dve.tensor_scalar(keep_f[:], keep_i[:], 0.0, None, ALU.not_equal))
                        link(dve.tensor_reduce(any_keep[:], keep_f[:], AX_X, ALU.max))
                elif name == "WG":
                    weigh(a, b)
                elif name == "O":
                    add_attention(a, b)
                elif name == "R0":
                    is_full(dve, PQ, "R0", b)
                    dve.tensor_tensor(LG[:, TB * b:TB * b + TB, :],
                                      bank[PQ][:, 0:TB * E0].rearrange("p (t e) -> p t e", t=TB),
                                      spread(rows[:, 2 * D:2 * D + E0], 1, TB), ALU.add).then_inc(read_out[PQ], 1)
                elif name == "RP":
                    probabilities()
                elif name == "CT":
                    if a < DIGITS:
                        one_digit(a)
                    else:
                        take()
                elif name == "GT":
                    gates0()
                elif name == "BD":
                    combine(a, b)
                elif name == "R1":
                    logits1(b)
                elif name == "GA":
                    gates1(b)
                elif name == "TG":
                    gates_to_rows(b)
                elif name == "SG":
                    gate_hidden(a, b)
                elif name == "DN1":
                    add_experts1(a, b)


_INS = ["x", "mask_tm", "mask_t", "weights", "tries_of", "gates", "w_up", "b_up", "w_down", "b_down", "w_up1", "w_dn1"]


def kernel(x, ctx_1024, mask_BxSxS2_if1, mask_BxSxS2_ik0, g_xattn, g_ffn, L0_xattn_Wq, L0_xattn_bq, L0_xattn_Wk,
           L0_xattn_bk, L0_xattn_Wv, L0_xattn_bv, L0_xattn_Wo, L0_xattn_bo, L0_ffn_Wr, L0_ffn_br, L0_ffn_W_up,
           L0_ffn_b_up, L0_ffn_W_down, L0_ffn_b_down, L1_xattn_W_kv, L1_xattn_b_kv, L1_xattn_W_q, L1_xattn_b_q,
           L1_xattn_W_o, L1_xattn_b_o, L1_ffn_shared_up, L1_ffn_shared_down, L1_ffn_routed_up, L1_ffn_routed_down,
           L1_ffn_router_w):
    import numpy as np
    import concourse.bacc as bacc
    from concourse.bass_utils import run_bass_kernel_spmd

    def on_rows(v):
        return np.broadcast_to(np.asarray(v).reshape(1, -1), (128, np.asarray(v).size))

    wkv = np.asarray(L1_xattn_W_kv).reshape(D, H, 2, DK)
    bkv = np.asarray(L1_xattn_b_kv).reshape(H, 2, DK)
    p, c = np.arange(128)[:, None], np.arange(128)[None, :]
    f32 = np.float32
    parts = {
        "wq0": np.asarray(L0_xattn_Wq).T, "wk0": np.asarray(L0_xattn_Wk).T, "wv0": np.asarray(L0_xattn_Wv).T,
        "wo0": np.asarray(L0_xattn_Wo).T, "ctxT": np.asarray(ctx_1024).reshape(B * SK, D).T,
        "wk1": wkv[:, :, 0].reshape(D, D), "wv1": wkv[:, :, 1].reshape(D, D), "wq1": np.asarray(L1_xattn_W_q),
        "wo1": np.asarray(L1_xattn_W_o), "wr0": np.asarray(L0_ffn_Wr), "wr1": np.asarray(L1_ffn_router_w).T,
        "cols": np.stack([np.asarray(L0_xattn_bq), np.asarray(L0_xattn_bk), np.asarray(L1_xattn_b_q),
                          bkv[:, 0].reshape(D)], 1),
        "rows": np.concatenate([on_rows(L0_xattn_bo), on_rows(L1_xattn_b_o), on_rows(L0_ffn_br),
                                on_rows(L0_xattn_bv), on_rows(bkv[:, 1].reshape(D))], 1),
        "ident": (p == c).astype(f32),
        "same_e": (p % E0 == c % E0).astype(f32),
        "before": ((p % E0 == c % E0) & (p // E0 < c // E0)).astype(f32),
        "headcol": (p // DK == c[:, :H]).astype(f32),
        "ones_blk": (p // SK == c[:, :HC * DK] // DK).astype(f32),
        "key32": (p - 64 == c[:, :SK]).astype(f32),
        "max16": ((p < 2 * H) & (p % H == c[:, :H])).astype(f32),
        "tile16": (p // E0 == c[:, :NT]).astype(f32),
        "gate16": ((p < 3 * R1) & (p % R1 == c[:, :R1])).astype(f32),
    }
    digit = np.arange(DIGITS)[:, None]
    tries_of = on_rows((np.arange(1, TRIES + 1)[None, :] << (BITS - RADIX_BITS * (digit + 1))).astype(np.int32))
    weights = np.concatenate([parts[n] for n in W_COLS], 1)
    b_up = np.zeros((128, NG, NF), f32)
    for k, (f0, fn) in enumerate(FCH):
        b_up[:fn, :, k] = np.asarray(L0_ffn_b_up)[:, f0:f0 + fn].T
    up1 = np.concatenate([np.asarray(L1_ffn_routed_up).reshape(R1 * EH, D),
                          np.asarray(L1_ffn_shared_up).reshape(-1, D)]).T
    dn1 = np.concatenate([np.asarray(L1_ffn_routed_down).transpose(0, 2, 1).reshape(R1 * EH, D),
                          np.asarray(L1_ffn_shared_down).transpose(0, 2, 1).reshape(-1, D)])
    masks = [np.asarray(m).reshape(B * S, SK) for m in (mask_BxSxS2_if1, mask_BxSxS2_ik0)]
    gx, gf = np.asarray(g_xattn), np.asarray(g_ffn)
    given = {
        "x": np.asarray(x).reshape(B * S, D), "mask_tm": masks[0], "mask_t": np.stack([m.T for m in masks]),
        "weights": weights, "tries_of": tries_of, "gates": on_rows(np.stack([gx[0], gf[0], gx[1], gf[1]])),
        "w_up": np.asarray(L0_ffn_W_up), "b_up": b_up, "w_down": np.asarray(L0_ffn_W_down),
        "b_down": np.tile(np.asarray(L0_ffn_b_down), (NT, 1)), "w_up1": up1,
        "w_dn1": dn1.reshape(CH1, 128, D).transpose(1, 0, 2),
    }
    nc = bacc.Bacc("TRN2", target_bir_lowering=False, num_devices=1)
    arrays, args = {}, []
    for name in _INS:
        a = np.ascontiguousarray(given[name])
        arrays[f"in_{name}"] = a
        args.append(nc.dram_tensor(f"in_{name}", a.shape, mybir.dt.from_np(a.dtype), kind="ExternalInput").ap())
    args.append(nc.dram_tensor("out_x", (B * S, D), F32, kind="ExternalOutput").ap())
    build(nc, *args)
    r = run_bass_kernel_spmd(nc, [arrays], core_ids=[0])
    return r.results[0]["out_x"].reshape(B, S, D)
```

```python
from contextlib import ExitStack

import concourse.bass as bass
from concourse import mybir
from concourse.alu_op_type import AluOpType as ALU

ACT = mybir.ActivationFunctionType
F32 = mybir.dt.float32
F32R = mybir.dt.float32r
BF16 = mybir.dt.bfloat16
I32 = mybir.dt.int32
AX_X = mybir.AxisListType.X

B, S, D, SK, H = 4, 512, 128, 32, 16
DK = D // H
TB = S // 128
NT = B * TB
HC = 4
NC = H // HC
E0, NG, FF = 8, 4, 341
TOPK0 = B * S // E0
FCH = [(0, 128), (128, 128), (256, FF - 256)]
NF = len(FCH)
R1, EH, TOP1 = 16, 64, 4
CH1 = R1 * EH // 128 + 1
LN_EPS = 1e-5
MASKED = -float(2 ** 66)
SCALE = float(DK) ** -0.5
BITS = 30
RADIX_BITS = 2
DIGITS = BITS // RADIX_BITS
TRIES = 2 ** RADIX_BITS - 1
AHEAD = 2

W_COLS = {}
_at = 0
for _n, _w in (("ident", 128), ("cols", 4), ("headcol", H), ("ctxT", B * SK), ("wk0", D),
               ("wq0", D), ("wv0", D), ("ones_blk", 32), ("key32", SK), ("max16", H), ("rows", 4 * D + E0),
               ("wo0", D), ("wo1", D), ("wk1", D), ("wv1", D), ("wq1", D), ("wr0", E0), ("wr1", R1),
               ("same_e", 128), ("before", 128), ("gate16", R1)):
    W_COLS[_n] = (_at, _w)
    _at += _w
NW = _at
W_PARTS = [0, W_COLS["wq0"][0], W_COLS["wo0"][0], NW]
EARLY = TB

TP, PQ, SM0, SM1, ST0, ST1, PV, SU = range(8)
DOWN_BANKS = [(SM0, SM1), (PV, SU)]
DOWN1_BANKS = [PV, SU]


ORDER = """
    LS:0:0 LA:0:0 LS:0:1 LS:0:2 K:0:0 V:0:0 LN:0:0 Q:0:0 LA:0:1 LS:0:3 SM:0:0 LN:0:1 K:1:0 SM:1:0 V:1:0 SM:2:0 SM:3:0
    Q:0:1 SM:0:1 NT:0:0 SM:1:1 LA:0:2 ST:0:0 LA:0:3 LN:0:2 PV:0:0 SM:2:1 WG:0:0 SM:3:1 Q:0:2 LN:0:3 SM:0:2 NT:0:1
    SM:1:2 O:0:0 LS:1:0 SM:2:2 LA:1:0 ST:0:1 SM:3:2 Q:0:3 LN:1:0 PV:0:1 NT:0:2 SM:0:3 XL:1:0 WG:0:1 ST:0:2 SM:1:3
    SM:2:3 UP0:0:0 PV:0:2 SM:3:3 O:0:1 WG:0:2 UP0:1:0 NT:0:3 LS:1:1 UP0:2:0 O:0:2 LS:1:2 ST:0:3 LA:1:2 PV:0:3 UP0:3:0
    R0:0:0 WG:0:3 UP0:4:0 LN:1:2 LA:1:1 O:0:3 LS:1:3 LA:1:3 UP0:5:0 UP0:6:0 LN:1:1 UP0:7:0 UP0:8:0 R0:0:1 UP0:9:0
    UP0:10:0 LN:1:3 R0:0:2 UP0:11:0 DN:0:0 XL:1:1 R0:0:3 DN:1:0 DN:2:0 RP:0:0 UP0:0:1 DN:3:0 CT:0:0 UP0:1:1 UP0:2:1
    DN:4:0 UP0:3:1 CT:1:0 DN:5:0 UP0:4:1 UP0:5:1 CT:2:0 DN:6:0 UP0:6:1 CT:3:0 DN:7:0 UP0:7:1 UP0:8:1 CT:4:0 DN:8:0
    DN:9:0 CT:5:0 UP0:9:1 DN:10:0 CT:6:0 DN:11:0 DN:12:0 CT:7:0 DN:13:0 UP0:10:1 CT:8:0 UP0:11:1 XL:1:2 DN:14:0
    DN:15:0 CT:9:0 DN:0:1 UP0:0:2 CT:10:0 UP0:1:2 DN:1:1 CT:11:0 UP0:2:2 DN:2:1 CT:12:0 UP0:3:2 DN:3:1 CT:13:0 UP0:4:2
    UP0:5:2 CT:14:0 UP0:6:2 UP0:7:2 CT:15:0 UP0:8:2 UP0:9:2 GT:0:0 DN:4:1 DN:5:1 DN:6:1 BD:0:0 BD:1:0 DN:7:1 BD:2:0
    BD:3:0 LS:2:0 UP0:10:2 LA:2:0 BD:0:1 BD:1:1 LN:2:0 Q:1:0 UP0:11:2 SM:4:0 SM:5:0 SM:6:0 SM:7:0 DN:8:1 NT:1:0 DN:9:1
    ST:1:0 PV:1:0 DN:10:1 WG:1:0 DN:11:1 BD:2:1 O:1:0 DN:12:1 DN:13:1 DN:14:1 DN:15:1 XL:1:3 BD:3:1 UP0:0:3 UP0:1:3
    LS:2:1 DN:0:2 LA:2:1 UP0:2:3 DN:1:2 DN:2:2 UP0:3:3 DN:3:2 DN:4:2 UP0:4:3 UP0:5:3 LS:3:0 LN:2:1 UP0:6:3 UP0:7:3
    BD:0:2 Q:1:1 DN:5:2 DN:6:2 SM:4:1 UP0:8:3 LA:3:0 UP0:9:3 SM:5:1 UP0:10:3 SM:6:1 LN:3:0 SM:7:1 UP0:11:3 DN:7:2
    DN:8:2 BD:1:2 NT:1:1 DN:9:2 R1:1:0 XL:3:0 GA:1:0 ST:1:1 PV:1:1 WG:1:1 DN:10:2 TG:1:0 DN:11:2 O:1:1 LS:3:1 UP1:0:0
    BD:2:2 UP1:1:0 SG:0:0 LA:3:1 SG:1:0 DN:12:2 SG:2:0 DN:13:2 SG:3:0 DN:14:2 SG:4:0 SG:5:0 DN:15:2 LN:3:1 BD:3:2
    UP1:2:0 SG:6:0 SG:7:0 DN1:0:0 R1:1:1 LS:2:2 GA:1:1 DN:0:3 DN:1:3 DN1:1:0 DN:2:3 LA:2:2 DN1:2:0 LN:2:2 XL:3:1
    DN:3:3 BD:0:3 Q:1:2 DN1:3:0 DN:4:3 SM:4:2 SM:5:2 DN:5:3 SM:6:2 SM:7:2 DN:6:3 DN:7:3 DN:8:3 NT:1:2 DN:9:3 ST:1:2
    BD:1:3 DN:10:3 DN:11:3 TG:1:1 UP1:0:1 BD:2:3 PV:1:2 SG:0:1 SG:1:1 WG:1:2 SG:2:1 UP1:1:1 SG:3:1 DN:12:3 SG:4:1
    SG:5:1 DN:13:3 DN:14:3 DN:15:3 BD:3:3 LS:2:3 UP1:2:1 SG:6:1 O:1:2 SG:7:1 LA:2:3 LS:3:2 LA:3:2 DN1:0:1 LN:2:3
    DN1:1:1 Q:1:3 LN:3:2 XL:3:2 SM:4:3 DN1:2:1 R1:1:2 GA:1:2 SM:5:3 DN1:3:1 UP1:0:2 SM:6:3 TG:1:2 SM:7:3 UP1:1:2
    NT:1:3 SG:0:2 SG:1:2 ST:1:3 PV:1:3 SG:2:2 SG:3:2 WG:1:3 SG:4:2 SG:5:2 O:1:3 LS:3:3 UP1:2:2 SG:6:2 SG:7:2 LA:3:3
    DN1:0:2 LN:3:3 XL:3:3 DN1:1:2 R1:1:3 GA:1:3 DN1:2:2 DN1:3:2 TG:1:3 UP1:0:3 SG:0:3 SG:1:3 UP1:1:3 SG:2:3 SG:3:3
    UP1:2:3 SG:4:3 SG:5:3 SG:6:3 SG:7:3 DN1:0:3 DN1:1:3 DN1:2:3 DN1:3:3
"""


def schedule():
    return [(name, int(a), int(b)) for name, a, b in (stage.split(":") for stage in ORDER.split())]


def bank_uses(stages):
    uses = {k: {} for k in range(8)}

    def use(k, *key):
        uses[k][key] = len(uses[k])

    for name, a, b in stages:
        if name == "LN":
            use(TP, name, a, b)
        elif name == "K":
            use(PQ, name, a)
        elif name == "V":
            use(PV, name, a)
        elif name in ("Q", "O"):
            use(PQ, name, a, b)
        elif name == "R0":
            use(PQ, name, b)
        elif name == "SM":
            use(SM0 + a % TB % 2, name, a // TB, b, a % TB)
        elif name == "NT":
            use(TP, name, a, b)
        elif name == "ST":
            for c in range(NC):
                use(ST0 + c % 2, name, a, b, c)
        elif name == "PV":
            use(PV, name, a, b)
            use(SU, name, a, b)
        elif name == "RP":
            use(TP, "P")
        elif name == "CT":
            use(PQ, "COUNT", a)
        elif name == "GT":
            use(TP, "G")
        elif name == "UP0":
            use(ST0 + a % 2, "UP0", b, a)
        elif name == "DN":
            t = TB * b + a // NG
            if a % 2 == 0:
                use(DOWN_BANKS[t % 2][a % NG // 2], "DN", t)
        elif name == "R1":
            use(PQ, name, b)
        elif name == "TG":
            use(TP, name, b)
        elif name == "UP1":
            for c in thirds(a):
                use(ST0 + c % 2, name, b, c)
        elif name == "SG":
            use(SM0 + a % 2, "GATE", b, a)
        elif name == "DN1":
            use(DOWN1_BANKS[a % 2], name, b, a)
    return uses


def thirds(part):
    return range(CH1 // 3 * part, CH1 // 3 * part + CH1 // 3)


def spread(ap, axis, n):
    ap = ap.unsqueeze(axis)
    shape = list(ap.shape)
    shape[axis] = n
    return ap.broadcast_to(shape)


def build(nc, x, mask_tm, mask_t, weights, tries_of, gates, w_up, b_up, w_down, b_down, w_up1, w_dn1, out):
    order = schedule()
    uses = bank_uses(order)
    nth_ln = {(a, b): n for n, (a, b) in enumerate([(a, b) for name, a, b in order if name == "LA"])}
    nth_var = {(a, b): n for n, (a, b) in enumerate([(a, b) for name, a, b in order if name == "LS"])}
    nth_att = {(a, b): n for n, (a, b) in enumerate([(a, b) for name, a, b in order if name == "Q"])}
    att = list(nth_att)

    with ExitStack() as ctx:
        def sb(name, shape, dt=F32):
            return ctx.enter_context(nc.sbuf_tensor(name, shape, dt))

        def sem(name):
            return ctx.enter_context(nc.semaphore(name))

        bank = [ctx.enter_context(nc.psum_tensor(f"bank{i}", [128, 512], F32)) for i in range(8)]

        W = sb("W", [128, NW])
        g_raw, g_tanh = sb("g_raw", [128, 4]), sb("g_tanh", [128, 4])
        bup = sb("bup", [128, NG, NF])
        wdn = sb("wdn", [128, NF, E0, D])
        wup_hi, wup_lo = sb("wup_hi", [128, NG, FF], F32R), sb("wup_lo", [128, NG, FF], F32R)
        wup1_hi, wup1_lo = sb("wup1_hi", [128, CH1 * 128], F32R), sb("wup1_lo", [128, CH1 * 128], F32R)
        XT_hi, XT_lo = sb("XT_hi", [128, S], F32R), sb("XT_lo", [128, S], F32R)
        wdn1 = sb("wdn1", [128, CH1, D])
        bk_s = sb("bk_s", [128, 2])
        ident_b = sb("ident_b", [128, 128], BF16)
        same_b, before_b = sb("same_b", [128, 128], BF16), sb("before_b", [128, 128], BF16)
        mask_rows, max_rows = sb("mask_rows", [128, H, SK], BF16), sb("max_rows", [128, H, SK], BF16)
        gate_rows = sb("gate_rows", [128, R1, EH], BF16)
        any_keep = sb("any_keep", [128, NT])
        X, XB = sb("X", [128, NT, D]), sb("XB", [128, 2, TB, D])
        XN, XT = sb("XN", [128, 2, TB, D]), sb("XT", [128, B, S])
        stats, mv = sb("stats", [128, NT, 6]), sb("mv", [128, NT, 2])
        vare, rstd, minus_half = sb("vare", [128, NT]), sb("rstd", [128, NT]), sb("minus_half", [128, TB])
        Q_hi, Q_lo = sb("Q_hi", [128, 2, S], F32R), sb("Q_lo", [128, 2, S], F32R)
        kcol = sb("kcol", [128, 2, B * SK])
        K_hi, K_lo = sb("K_hi", [128, B, H * SK], F32R), sb("K_lo", [128, B, H * SK], F32R)
        VB = sb("VB", [128, 2, B * NC, 32])
        shift = sb("shift", [128, B, S], BF16)
        mx, nm = sb("mx", [128, NT, H]), sb("nm", [128, 2, TB, 2, H], BF16)
        PT = sb("PT", [128, 2, NC, S])
        early = PT[:].rearrange("p n c s -> p (n c) s").rearrange("p (t h) s -> p t h s", t=EARLY)
        AT = sb("AT", [128, 2, S])
        LG, P0 = sb("LG", [128, NT, E0]), sb("P0", [128, NT, E0])
        lmax, lsm, lrc = sb("lmax", [128, NT]), sb("lsm", [128, NT]), sb("lrc", [128, NT])
        PRT, GT = sb("PRT", [128, 128]), sb("GT", [128, 128])
        eq, run, gt = (sb(n, [128, 128]) for n in ("eq", "run", "gt"))
        count, left = sb("count", [128, TRIES], BF16), sb("left", [128, 2])
        tries, reached = sb("tries", [128, DIGITS, TRIES], I32), sb("reached", [128, TRIES])
        cand, digit, digit_f = sb("cand", [128, 1], I32), sb("digit", [128, 2], I32), sb("digit_f", [128, 2])
        G0 = sb("G0", [128, NT, E0])
        MID = sb("MID", [128, NG * NF, AHEAD, S])
        ctx4 = MID[:, 0, 0, :].rearrange("p (b q) -> p b q", b=B)
        wup = MID[:, NF:NF + 2, :, :].rearrange("p i a s -> p (i a s)")[:, 0:NG * FF]
        acc = sb("acc", [128, 2, D])
        lg1, p1 = sb("lg1", [128, TB, R1]), sb("p1", [128, TB, R1 + 4])
        m1, s1, r1 = sb("m1", [128, TB]), sb("s1", [128, TB]), sb("r1", [128, TB])
        top8, take8 = sb("top8", [128, TB, 8]), sb("take8", [128, TB, 8])
        rest, gate = sb("rest", [128, TB, R1 + 4]), sb("gate", [128, TB, R1])
        gres, g3 = sb("gres", [128, TB, R1]), sb("g3", [128, TB, 3, R1], BF16)
        gT = sb("gT", [128, S], BF16)
        HG = sb("HG", [128, CH1, S])
        kcol_hi = gT[:, 0:2 * B * SK].bitcast(F32)
        mask_i = HG[:, 0:B, :].rearrange("p b s -> p (b s)").bitcast(I32)
        keep_i = HG[:, B, :].rearrange("p (t k) -> p t k", t=NT).bitcast(I32)
        wup1 = HG[:, B + 2:CH1, :].rearrange("p c s -> p (c s)")[:, 0:CH1 * 128]
        keep_f = HG[:, B + 1, :].rearrange("p (t k) -> p t k", t=NT)

        def w(name):
            at, n = W_COLS[name]
            return W[:, at:at + n]

        cols, rows, ident = w("cols"), w("rows"), w("ident")
        wo = [w("wo0"), w("wo1")]
        bo_g = [rows[:, D * layer:D * layer + D] for layer in range(2)]
        bv = [rows[:, 2 * D + E0 + D * layer:3 * D + E0 + D * layer] for layer in range(2)]
        x_dram = x.rearrange("(t p) h -> p t h", p=128)
        out_dram = out.rearrange("(t p) h -> p t h", p=128)

        filled = [sem(f"bank{i}_filled") for i in range(8)]
        read_out = [sem(f"bank{i}_read_out") for i in range(8)]

        def may_fill(eng, k, *key):
            if uses[k][key] > 0:
                eng.wait_ge(read_out[k], uses[k][key])

        def is_full(eng, k, *key):
            eng.wait_ge(filled[k], uses[k][key] + 1)

        def is_read(eng, k, *key):
            eng.wait_ge(read_out[k], uses[k][key] + 1)

        x_in = [sem(f"x_in{b}") for b in range(B)]
        tries_in, g_in, keep_in, up_in, up1_in = (sem(n) for n in ("tries_in", "g_in", "keep_in", "up_in", "up1_in"))
        w_in = [sem(f"w_in{n}") for n in range(3)]
        mask_in = [sem("mask_in0"), sem("mask_in1")]
        dn_in = sem("dn_in")
        tanh_done, mask_done = sem("tanh_done"), [sem("mask_done0"), sem("mask_done1")]
        pool_const, pool_chain, vec_const = sem("pool_const"), sem("pool_chain"), sem("vec_const")
        var_done, rstd_done, xn_done = sem("var_done"), sem("rstd_done"), sem("xn_done")
        keys_done, q_hi_done = sem("keys_done"), sem("q_hi_done")
        nm_done = sem("nm_done")
        rs_done, xb_done = sem("rs_done"), sem("xb_done")
        vec_chain = sem("vec_chain")
        lgs_done, e0_done, count_done = sem("lgs_done"), sem("e0_done"), sem("count_done")
        prob_done, gt_done, ones_done = sem("prob_done"), sem("gt_done"), sem("ones_done")
        vb_done, e1_done, g3_done, experts0_done = (
            sem(n) for n in ("vb_done", "e1_done", "g3_done", "experts0_done"))
        parts_done, up_split = [sem("parts_done0"), sem("parts_done1")], sem("up_split")
        y_out = sem("y_out")

        HALF, BK, MASK_ROWS, MAX_ROWS, WO, BO, GATE_ROWS, WDN1, TAKE = range(1, 10)

        def split_keys(eng, layer, link):
            k = kcol[:, layer, :]
            link(eng.tensor_copy(kcol_hi.bitcast(F32R), k))
            link(eng.tensor_tensor(k, k, kcol_hi, ALU.subtract))

        def place_keys(eng, layer, b, done):
            for out, col in ((K_hi, kcol_hi), (K_lo, kcol[:, layer, :])):
                eng.tensor_tensor(out[:, b, :].rearrange("p (h k) -> p h k", h=H), spread(w("headcol"), 2, SK),
                                  spread(col[:, SK * b:SK * b + SK], 1, H), ALU.mult).then_inc(done, 1)

        block = ctx.enter_context(nc.Block())

        @block.sync
        def _(sp):
            for n in range(3):
                part = slice(W_PARTS[n], W_PARTS[n + 1])
                sp.dma_start(W[:, part], weights[:, part]).then_inc(w_in[n], 16)
            sp.dma_start(mask_i[64:96, :], mask_t[0]).then_inc(mask_in[0], 16)
            for b in range(1, B):
                t = slice(TB * b, TB * b + TB)
                sp.dma_start(X[:, t, :], x_dram[:, t, :]).then_inc(x_in[b], 16)
            sp.dma_start(keep_i[:], mask_tm.rearrange("(t p) k -> p t k", p=128)).then_inc(keep_in, 16)
            sp.dma_start(tries[:], tries_of).then_inc(tries_in, 16)
            sp.dma_start(wup.rearrange("p (g f) -> p g f", g=NG), w_up.rearrange("g h f -> h g f")).then_inc(up_in, 16)
            sp.dma_start(bup[:], b_up).then_inc(up_in, 16)
            sp.dma_start(wdn[FCH[-1][1]:FCH[-1][1] + 1, NF - 1, :, :], b_down.unsqueeze(0)).then_inc(dn_in, 16)
            for k, (f0, fn) in enumerate(FCH):
                sp.dma_start(wdn[0:fn, k, :, :], w_down[:, f0:f0 + fn, :].rearrange("e f h -> f e h"))\
                    .then_inc(dn_in, 16)
            sp.dma_start(wup1, w_up1).then_inc(up1_in, 16)
            sp.dma_start(wdn1[:], w_dn1).then_inc(up1_in, 16)
            sp.wait_ge(mask_done[0], B)
            sp.dma_start(mask_i[64:96, :], mask_t[1]).then_inc(mask_in[1], 16)
            for b in range(B):
                for j in range(0, TB, 2):
                    is_read(sp, DOWN1_BANKS[0], "DN1", b, j)
                    is_read(sp, DOWN1_BANKS[1], "DN1", b, j + 1)
                    t = slice(TB * b + j, TB * b + j + 2)
                    sp.dma_start(out_dram[:, t, :], X[:, t, :]).then_inc(y_out, 16)
            sp.wait_ge(y_out, 16 * B * TB // 2)

        @block.gpsimd
        def _(pool):
            links = [0]

            def link(ins):
                links[0] += 1
                ins.then_inc(pool_chain, 1)
                pool.wait_ge(pool_chain, links[0])

            def rstd_of(a, b):
                t = slice(TB * b, TB * b + TB)
                pool.wait_ge(var_done, nth_var[(a, b)] + 1)
                link(pool.tensor_scalar(vare[:, t], mv[:, t, 1], LN_EPS, None, ALU.add))
                pool.tensor_tensor(rstd[:, t], vare[:, t], minus_half[:], ALU.pow).then_inc(rstd_done, 1)

            def x_plus_bias(layer, b):
                if layer == 0:
                    pool.wait_ge(x_in[b], 16)
                else:
                    pool.wait_ge(experts0_done, TB * b + TB)
                n = nth_att[(layer, b)]
                if n >= 2:
                    is_read(pool, PQ, "O", *att[n - 2])
                pool.tensor_tensor(XB[:, n % 2, :, :], X[:, TB * b:TB * b + TB, :], spread(bo_g[layer], 1, TB),
                                   ALU.add).then_inc(xb_done, 1)

            def operands_of_layer_1():
                is_read(pool, PQ, "K", 1)
                is_read(pool, ST1, "ST", 0, B - 1, NC - 1)
                split_keys(pool, 1, link)
                for b in range(B):
                    place_keys(pool, 1, b, keys_done)
                pool.tensor_copy(gate_rows[:], spread(w("gate16"), 2, EH)).then_inc(pool_const, 1)
                pool.wait_ge(up1_in, 32)
                link(pool.tensor_copy(wup1_hi[:], wup1))
                link(pool.tensor_tensor(wup1_lo[:], wup1, wup1_hi[:].bitcast(F32), ALU.subtract))
                pool.tensor_scalar(wdn1[:].rearrange("p c h -> p (c h)"), wdn1[:].rearrange("p c h -> p (c h)"),
                                   g_tanh[:, 3:4], None, ALU.mult).then_inc(pool_const, 1)
                pool.memset(take8[:], -1.0)
                pool.memset(p1[:], -1.0).then_inc(pool_const, 1)

            pool.memset(minus_half[:], -0.5).then_inc(pool_const, 1)
            pool.wait_ge(w_in[0], 16)
            pool.tensor_scalar(bk_s[:], cols[:, 1:4:2], SCALE, None, ALU.mult).then_inc(pool_const, 1)
            rstd_of(0, 0)
            pool.wait_ge(w_in[1], 16)
            pool.tensor_copy(mask_rows[:], spread(w("key32"), 1, H)).then_inc(pool_const, 1)
            pool.tensor_copy(max_rows[:], spread(w("max16"), 2, SK)).then_inc(pool_const, 1)
            rstd_of(0, 1)
            pool.wait_ge(tanh_done, 1)
            pool.wait_ge(w_in[2], 16)
            pool.tensor_scalar(wo[0], wo[0], g_tanh[:, 0:1], None, ALU.mult)
            pool.tensor_scalar(wo[1], wo[1], g_tanh[:, 2:3], None, ALU.mult).then_inc(pool_const, 1)
            pool.tensor_scalar(bo_g[0], bo_g[0], g_tanh[:, 0:1], None, ALU.mult)
            pool.tensor_scalar(bo_g[1], bo_g[1], g_tanh[:, 2:3], None, ALU.mult).then_inc(pool_const, 1)
            pool.wait_ge(pool_const, BO)

            last = FCH[-1][1] // 32 * 32
            pool.memset(MID[:].rearrange("p (g f) a s -> p g f (a s)", f=NF)[last:last + 32, :, NF - 1, :], 1.0)\
                .then_inc(ones_done, 1)
            pool.wait_ge(ones_done, 1)
            for name, a, b in order:
                if name == "LS" and (a, b) not in ((0, 0), (0, 1)):
                    rstd_of(a, b)
                if name == "Q" and a == 0:
                    x_plus_bias(0, b)
                if name == "LS" and a == 2:
                    x_plus_bias(1, b)
                if (name, a, b) == ("PV", 0, 0):
                    pool.wait_ge(up_in, 32)
                    hi, lo = (t[:].rearrange("p g f -> p (g f)") for t in (wup_hi, wup_lo))
                    link(pool.tensor_copy(hi, wup))
                    pool.tensor_tensor(lo, wup, hi.bitcast(F32), ALU.subtract).then_inc(up_split, 1)
                    pool.wait_ge(up_split, 1)
                if name == "RP":
                    operands_of_layer_1()

        @block.scalar
        def _(act):
            act.dma_start(X[:, 0:TB, :], x_dram[:, 0:TB, :]).then_inc(x_in[0], 16)
            act.dma_start(g_raw[:], gates).then_inc(g_in, 16)
            act.preload_act_table_set("exp_and_others")
            act.wait_ge(g_in, 16)
            act.activation(g_tanh[:], g_raw[:], ACT.Tanh).then_inc(tanh_done, 1)
            act.preload_act_table_set("natural_log_exp_and_others")
            act.wait_ge(pool_const, BK)

            table = ["natural_log_exp_and_others"]

            def tables(name):
                if table[0] != name:
                    act.preload_act_table_set(name)
                    table[0] = name

            def keys(layer):
                is_full(act, PQ, "K", layer)
                act.activation(kcol[:, layer, :], bank[PQ][:, 0:B * SK], ACT.Identity, bias=bk_s[:, layer:layer + 1],
                               scale=SCALE).then_inc(read_out[PQ], 1)

            def normalised(a, b):
                is_full(act, TP, "LN", a, b)
                act.activation(XT[:, b, :], bank[TP][:], ACT.Copy).then_inc(read_out[TP], 1)

            def queries(layer, b):
                is_full(act, PQ, "Q", layer, b)
                n = nth_att[(layer, b)]
                if n >= 2:
                    is_full(act, ST1, "ST", *att[n - 2], NC - 1)
                act.activation(Q_hi[:, n % 2, :], bank[PQ][:], ACT.Identity,
                               bias=cols[:, 2 * layer:2 * layer + 1]).then_inc(q_hi_done, 1)

            def exps(layer, b):
                n = nth_att[(layer, b)]
                tables("natural_log_exp_and_others")
                if layer == 1 and b < 2:
                    act.wait_ge(experts0_done, EARLY)
                if n >= 2:
                    is_full(act, SU, "PV", *att[n - 2])
                for c in range(NC):
                    k = ST0 + c % 2
                    is_full(act, k, "ST", layer, b, c)
                    act.activation(PT[:, n % 2, c, :], bank[k][:], ACT.Exp).then_inc(read_out[k], 1)

            def inverse_sums(layer, b):
                n = nth_att[(layer, b)]
                tables("natural_log_exp_and_others")
                is_full(act, SU, "PV", layer, b)
                if n >= 2:
                    is_full(act, PQ, "O", *att[n - 2])
                inverse = AT[:, n % 2, :]
                act.activation(inverse, bank[SU][:], ACT.Ln).then_inc(read_out[SU], 1)
                is_read(act, SU, "PV", layer, b)
                act.activation(inverse, inverse, ACT.Exp, scale=-1.0).then_inc(rs_done, 1)

            def hidden0(b, i):
                g, (f0, fn) = i // NF, FCH[i % NF]
                tables("silu_and_others")
                if b >= AHEAD and i == 0:
                    is_full(act, DOWN_BANKS[1][1], "DN", TB * (b - AHEAD) + TB - 1)
                k = ST0 + i % 2
                is_full(act, k, "UP0", b, i)
                act.activation(MID[0:fn, i, b % AHEAD, :], bank[k][0:fn, :], ACT.Silu,
                               bias=bup[0:fn, g, i % NF:i % NF + 1]).then_inc(read_out[k], 1)

            def keep_outputs(t):
                if t == 0:
                    is_full(act, SU, "PV", 0, B - 1)
                    is_full(act, SU, "PV", 0, B - 2)
                for half, k in enumerate(DOWN_BANKS[t % 2]):
                    is_full(act, k, "DN", t)
                    act.activation(early[:, t, half, :], bank[k][:], ACT.Copy).then_inc(read_out[k], 1)

            for name, a, b in order:
                if name == "K":
                    keys(a)
                elif name == "LN":
                    normalised(a, b)
                elif name == "Q":
                    queries(a, b)
                elif name == "DN" and a % NG == NG - 1 and TB * b + a // NG < EARLY:
                    keep_outputs(TB * b + a // NG)
                elif name == "ST":
                    exps(a, b)
                elif name == "PV":
                    inverse_sums(a, b)
                elif name == "RP":
                    tables("natural_log_exp_and_others")
                    act.wait_ge(lgs_done, 1)
                    act.activation(P0[:].rearrange("p t e -> p (t e)"), LG[:].rearrange("p t e -> p (t e)"), ACT.Exp)\
                        .then_inc(e0_done, 1)
                elif name == "UP0":
                    if (a, b) == (0, 0):
                        act.wait_ge(up_in, 32)
                        act.wait_ge(ones_done, 1)
                        act.wait_ge(up_split, 1)
                        is_full(act, PV, "V", 1)
                    hidden0(b, a)
                elif name == "R1":
                    tables("natural_log_exp_and_others")
                    is_read(act, PQ, "R1", b)
                    act.activation(p1[:, :, 0:R1], lg1[:], ACT.Exp).then_inc(e1_done, 1)
                elif name == "UP1":
                    tables("gelu_and_others")
                    for c in thirds(a):
                        k = ST0 + c % 2
                        is_full(act, k, "UP1", b, c)
                        if b == 0 and c == 0:
                            act.wait_ge(mask_done[1], 1)
                        if b >= 1 and c == 0:
                            is_full(act, DOWN1_BANKS[1], "DN1", b - 1, TB - 1)
                        act.activation(HG[:, c, :], bank[k][:], ACT.Gelu).then_inc(read_out[k], 1)

        @block.tensor
        def _(pe):
            def fill(k):
                return lambda ins: ins.then_inc(filled[k], 1)

            def turn(a, b):
                may_fill(pe, TP, "LN", a, b)
                n = nth_ln[(a, b)]
                for j in range(TB):
                    pe.wait_ge(xn_done, TB * n + j + 1)
                    ins = pe.transpose(bank[TP][:, 128 * j:128 * j + 128], XN[:, n % 2, j, :], ident)
                fill(TP)(ins)

            def keys(layer):
                pe.wait_ge(w_in[2 * layer], 16)
                may_fill(pe, PQ, "K", layer)
                fill(PQ)(pe.matmul(bank[PQ][:, 0:B * SK], w(f"wk{layer}"), w("ctxT"), start=True, stop=True))

            def values(layer):
                pe.wait_ge(w_in[2 * layer], 16)
                may_fill(pe, PV, "V", layer)
                if layer == 0:
                    pe.wait_ge(vec_const, 1)
                    pe.wait_ge(w_in[1], 16)
                for b in range(B):
                    o = bank[PV][:, D * b:D * b + D]
                    ins = pe.matmul(o, ctx4[:, b, :], w(f"wv{layer}"), start=True, stop=True)
                fill(PV)(ins)

            def queries(layer, b):
                may_fill(pe, PQ, "Q", layer, b)
                if (layer, b) == (0, 0):
                    pe.wait_ge(w_in[1], 16)
                is_read(pe, TP, "LN", 2 * layer, b)
                fill(PQ)(pe.matmul(bank[PQ][:], w(f"wq{layer}"), XT[:, b, :], start=True, stop=True))

            def scores_for_max(part, b):
                layer, j = divmod(part, TB)
                n = nth_att[(layer, b)]
                pe.wait_ge(q_hi_done, n + 1)
                if j == 0:
                    pe.wait_ge(keys_done, 2 * (b + 1 if layer == 0 else 2 * B))
                    pe.wait_ge(mask_done[layer], b + 1 if layer == 0 else 1)
                    pe.wait_ge(pool_const, MASK_ROWS)
                k = SM0 + j % 2
                may_fill(pe, k, "SM", layer, b, j)
                t = slice(128 * j, 128 * j + 128)
                pe.matmul(bank[k][:], Q_hi[:, n % 2, t], K_hi[:, b, :], start=True, stop=False)
                fill(k)(pe.matmul(bank[k][:], shift[:, b, t], mask_rows[:].rearrange("p h k -> p (h k)"),
                                  start=False, stop=True))

            def turn_max(layer, b):
                n = nth_att[(layer, b)]
                may_fill(pe, TP, "NT", layer, b)
                pe.wait_ge(nm_done, n + 1)
                pe.wait_ge(vec_const, 2)
                o = bank[TP][:].bitcast(BF16)
                for j in range(TB):
                    ins = pe.transpose(o[0:2 * H, 128 * j:128 * j + 128],
                                       nm[:, n % 2, j, :, :].rearrange("p a h -> p (a h)"), ident_b[:])
                fill(TP)(ins)

            def scores(layer, b):
                n = nth_att[(layer, b)]
                is_read(pe, PQ, "Q", layer, b)
                pe.wait_ge(pool_const, MAX_ROWS)
                for c in range(NC):
                    k = ST0 + c % 2
                    may_fill(pe, k, "ST", layer, b, c)
                    r = slice(128 * c, 128 * c + 128)
                    pe.matmul(bank[k][:], K_hi[:, b, r], Q_hi[:, n % 2, :], start=True, stop=False)
                    pe.matmul(bank[k][:], K_lo[:, b, r], Q_hi[:, n % 2, :], start=False, stop=False)
                    pe.matmul(bank[k][:], K_hi[:, b, r], Q_lo[:, n % 2, :], start=False, stop=False)
                    if c == 0:
                        is_read(pe, TP, "NT", layer, b)
                    pe.matmul(bank[k][:], mask_rows[:].rearrange("p h k -> p (h k)")[:, r], shift[:, b, :],
                              start=False, stop=False)
                    fill(k)(pe.matmul(bank[k][:], max_rows[:].rearrange("p h k -> p (h k)")[:, r], shift[:, b, :],
                                      start=False, stop=True))

            def attend(layer, b):
                n = nth_att[(layer, b)]
                may_fill(pe, PV, "PV", layer, b)
                may_fill(pe, SU, "PV", layer, b)
                pe.wait_ge(vb_done, layer + 1)
                for c in range(NC):
                    is_read(pe, ST0 + c % 2, "ST", layer, b, c)
                    ins = pe.matmul(bank[PV][32 * c:32 * c + 32, :], VB[:, layer, NC * b + c, :], PT[:, n % 2, c, :],
                                    start=True, stop=True, tile_position=(0, 32 * c))
                fill(PV)(ins)
                for c in range(NC):
                    ins = pe.matmul(bank[SU][32 * c:32 * c + 32, :], w("ones_blk"), PT[:, n % 2, c, :],
                                    start=True, stop=True, tile_position=(0, 32 * c))
                fill(SU)(ins)

            def project(layer, b):
                n = nth_att[(layer, b)]
                may_fill(pe, PQ, "O", layer, b)
                is_read(pe, PV, "PV", layer, b)
                pe.wait_ge(pool_const, WO)
                for j in range(TB):
                    ins = pe.matmul(bank[PQ][:, D * j:D * j + D], AT[:, n % 2, 128 * j:128 * j + 128], wo[layer],
                                    start=True, stop=True)
                fill(PQ)(ins)

            def route_logits(b, key, weight, width, ln):
                may_fill(pe, PQ, key, b)
                is_read(pe, TP, "LN", ln, b)
                for j in range(TB):
                    ins = pe.matmul(bank[PQ][:, width * j:width * j + width], XT[:, b, 128 * j:128 * j + 128],
                                    w(weight), start=True, stop=True)
                fill(PQ)(ins)

            def up0(b, i):
                g, (f0, fn) = i // NF, FCH[i % NF]
                k = ST0 + i % 2
                may_fill(pe, k, "UP0", b, i)
                if i == 0:
                    pe.wait_ge(parts_done[0], b + 1)
                hi, lo = wup_hi[:, g, f0:f0 + fn], wup_lo[:, g, f0:f0 + fn]
                pe.matmul(bank[k][0:fn, :], hi, XT_hi[:], start=True, stop=False)
                pe.matmul(bank[k][0:fn, :], lo, XT_hi[:], start=False, stop=False)
                fill(k)(pe.matmul(bank[k][0:fn, :], hi, XT_lo[:], start=False, stop=True))

            def down0(part, b):
                j, g = divmod(part, NG)
                t = TB * b + j
                k = DOWN_BANKS[t % 2][g // 2]
                if g % 2 == 0:
                    may_fill(pe, k, "DN", t)
                for f, (f0, fn) in enumerate(FCH):
                    if j == 0:
                        is_read(pe, ST0 + (NF * g + f) % 2, "UP0", b, NF * g + f)
                    rows_in = fn + 1 if f == NF - 1 else fn
                    ins = pe.matmul(bank[k][:, 2 * D * (g % 2):2 * D * (g % 2) + 2 * D],
                                    MID[0:rows_in, NF * g + f, b % AHEAD, 128 * j:128 * j + 128],
                                    wdn[0:rows_in, f, 2 * g:2 * g + 2, :].rearrange("p e h -> p (e h)"),
                                    start=(f == 0), stop=(f == NF - 1))
                if g % 2 == 1:
                    fill(k)(ins)

            def count_all_tiles(i):
                may_fill(pe, PQ, "COUNT", i)
                pe.wait_ge(count_done, i + 1)
                if i < DIGITS:
                    fill(PQ)(pe.matmul(bank[PQ][:, 0:TRIES], same_b[:], count[:, 0:TRIES], start=True, stop=True))
                else:
                    pe.matmul(bank[PQ][:, 0:1], same_b[:], count[:, 0:1], start=True, stop=True)
                    fill(PQ)(pe.matmul(bank[PQ][:, 1:2], before_b[:], count[:, 1:2], start=True, stop=True))

            def turn_gates(b):
                may_fill(pe, TP, "TG", b)
                pe.wait_ge(g3_done, b + 1)
                o = bank[TP][:].bitcast(BF16)
                for j in range(TB):
                    ins = pe.transpose(o[0:3 * R1, 128 * j:128 * j + 128],
                                       g3[:, j, :, :].rearrange("p a r -> p (a r)"), ident_b[:])
                fill(TP)(ins)

            def up1(part, b):
                pe.wait_ge(parts_done[1], b + 1)
                for c in thirds(part):
                    k = ST0 + c % 2
                    may_fill(pe, k, "UP1", b, c)
                    rows = slice(128 * c, 128 * c + 128)
                    pe.matmul(bank[k][:], wup1_hi[:, rows], XT_hi[:], start=True, stop=False)
                    pe.matmul(bank[k][:], wup1_lo[:, rows], XT_hi[:], start=False, stop=False)
                    fill(k)(pe.matmul(bank[k][:], wup1_hi[:, rows], XT_lo[:], start=False, stop=True))

            def spread_gate(b, c):
                k = SM0 + c % 2
                may_fill(pe, k, "GATE", b, c)
                is_read(pe, TP, "TG", b)
                fill(k)(pe.matmul(bank[k][:], gate_rows[0:3 * R1, 2 * c:2 * c + 2, :].rearrange("p r e -> p (r e)"),
                                  gT[0:3 * R1, :], start=True, stop=True))

            def down1(j, b):
                k = DOWN1_BANKS[j % 2]
                may_fill(pe, k, "DN1", b, j)
                for c in range(CH1):
                    if j == 0 and c < CH1 - 1:
                        is_read(pe, SM0 + c % 2, "GATE", b, c)
                    elif j == 0:
                        is_read(pe, ST0 + c % 2, "UP1", b, c)
                    ins = pe.matmul(bank[k][:, 0:D], HG[:, c, 128 * j:128 * j + 128], wdn1[:, c, :],
                                    start=(c == 0), stop=(c == CH1 - 1))
                fill(k)(ins)

            for name, a, b in order:
                if name == "K":
                    keys(a)
                elif name == "V":
                    values(a)
                elif name == "LN":
                    turn(a, b)
                elif name == "Q":
                    queries(a, b)
                elif name == "SM":
                    scores_for_max(a, b)
                elif name == "NT":
                    turn_max(a, b)
                elif name == "ST":
                    scores(a, b)
                elif name == "PV":
                    attend(a, b)
                elif name == "O":
                    project(a, b)
                elif name == "R0":
                    route_logits(b, "R0", "wr0", E0, 1)
                elif name == "UP0":
                    if (a, b) == (0, 0):
                        pe.wait_ge(up_split, 1)
                    up0(b, a)
                elif name == "RP":
                    may_fill(pe, TP, "P")
                    pe.wait_ge(prob_done, 1)
                    fill(TP)(pe.transpose(bank[TP][:, 0:128], P0[:].rearrange("p t e -> p (t e)"), ident))
                elif name == "CT":
                    count_all_tiles(a)
                elif name == "GT":
                    may_fill(pe, TP, "G")
                    pe.wait_ge(gt_done, 1)
                    fill(TP)(pe.transpose(bank[TP][:, 0:128], GT[:], ident))
                elif name == "DN":
                    if (a, b) == (0, 0):
                        pe.wait_ge(dn_in, 16 * (1 + NF))
                    down0(a, b)
                elif name == "R1":
                    route_logits(b, "R1", "wr1", R1, 3)
                elif name == "UP1":
                    if b == 0 and a == 0:
                        pe.wait_ge(up1_in, 32)
                        pe.wait_ge(pool_const, WDN1)
                    up1(a, b)
                elif name == "TG":
                    turn_gates(b)
                elif name == "SG":
                    spread_gate(b, a)
                elif name == "DN1":
                    down1(a, b)

        @block.vector
        def _(dve):
            links = [0]

            def link(ins):
                links[0] += 1
                ins.then_inc(vec_chain, 1)
                dve.wait_ge(vec_chain, links[0])

            def statistics(a, b):
                t0 = TB * b
                if (a, b) in ((0, 0), (0, 1), (0, 2), (0, 3)):
                    dve.wait_ge(x_in[b], 16)
                elif a == 1:
                    is_read(dve, PQ, "O", 0, b)
                elif a == 2:
                    dve.wait_ge(experts0_done, t0 + TB)
                elif a == 3:
                    is_read(dve, PQ, "O", 1, b)
                for j in range(TB):
                    ins = dve.bn_stats(stats[:, t0 + j, :], X[:, t0 + j, :])
                link(ins)
                for j in range(TB):
                    ins = dve.bn_aggr(mv[:, t0 + j, :], stats[:, t0 + j, :])
                ins.then_inc(var_done, 1)

            def normalise(a, b):
                n = nth_ln[(a, b)]
                dve.wait_ge(var_done, nth_var[(a, b)] + 1)
                dve.wait_ge(rstd_done, nth_var[(a, b)] + 1)
                if n >= 2:
                    is_full(dve, TP, "LN", *list(nth_ln)[n - 2])
                for j in range(TB):
                    t = TB * b + j
                    dve.tensor_scalar(XN[:, n % 2, j, :], X[:, t, :], mv[:, t, 0:1], rstd[:, t:t + 1],
                                      ALU.subtract, ALU.mult).then_inc(xn_done, 1)

            def queries(layer, b):
                n = nth_att[(layer, b)]
                is_full(dve, PQ, "Q", layer, b)
                dve.wait_ge(q_hi_done, n + 1)
                dve.scalar_tensor_tensor(Q_lo[:, n % 2, :], bank[PQ][:], cols[:, 2 * layer:2 * layer + 1],
                                         Q_hi[:, n % 2, :].bitcast(F32), ALU.add, ALU.subtract)\
                    .then_inc(read_out[PQ], 1)

            def maxima(part, b):
                layer, j = divmod(part, TB)
                n, t0 = nth_att[(layer, b)], TB * b
                k = SM0 + j % 2
                is_full(dve, k, "SM", layer, b, j)
                dve.tensor_reduce(mx[:, t0 + j, :], bank[k][:].rearrange("p (h k) -> p h k", h=H), AX_X, ALU.max)\
                    .then_inc(read_out[k], 1)
                if j < TB - 1:
                    return
                is_read(dve, SM0, "SM", layer, b, TB - 2)
                is_read(dve, SM1, "SM", layer, b, TB - 1)
                m = mx[:, t0:t0 + TB, :]
                link(dve.tensor_scalar(nm[:, n % 2, :, 0, :], m, -1.0, None, ALU.mult))
                dve.scalar_tensor_tensor(nm[:, n % 2, :, 1, :], m, -1.0, nm[:, n % 2, :, 0, :], ALU.mult,
                                         ALU.subtract).then_inc(nm_done, 1)

            def max_to_rows(layer, b):
                is_full(dve, TP, "NT", layer, b)
                dve.tensor_copy(shift[0:2 * H, b, :], bank[TP][:].bitcast(BF16)[0:2 * H, 0:S])\
                    .then_inc(read_out[TP], 1)

            def weigh(layer, b):
                n = nth_att[(layer, b)]
                is_full(dve, PV, "PV", layer, b)
                dve.wait_ge(rs_done, n + 1)
                dve.tensor_tensor(AT[:, n % 2, :], bank[PV][:], AT[:, n % 2, :], ALU.mult).then_inc(read_out[PV], 1)

            def add_attention(layer, b):
                n = nth_att[(layer, b)]
                is_full(dve, PQ, "O", layer, b)
                dve.wait_ge(xb_done, n + 1)
                if layer == 0:
                    for j in range(TB):
                        t = TB * b + j
                        ins = dve.scalar_tensor_tensor(X[:, t, :], bank[PQ][:, D * j:D * j + D], any_keep[:, t:t + 1],
                                                       XB[:, n % 2, j, :], ALU.mult, ALU.add)
                else:
                    ins = dve.tensor_tensor(X[:, TB * b:TB * b + TB, :].rearrange("p t h -> p (t h)"), bank[PQ][:],
                                            XB[:, n % 2, :, :].rearrange("p t h -> p (t h)"), ALU.add)
                ins.then_inc(read_out[PQ], 1)

            def combine(j, b):
                t = TB * b + j
                banks = DOWN_BANKS[t % 2]
                sums = [acc[:, 0, :], acc[:, 1, :]]
                is_read(dve, PQ, "O", 0, b)
                if t > 0:
                    dve.wait_ge(experts0_done, t)
                done = links[0]
                for e in range(E0 // 2):
                    for half, k in ((1, banks[1]), (0, banks[0])):
                        out = sums[half]
                        part = early[:, t, half, D * e:D * e + D] if t < EARLY else bank[k][:, D * e:D * e + D]
                        gate = G0[:, t, E0 // 2 * half + e:E0 // 2 * half + e + 1]
                        if e == 0 and t < EARLY:
                            is_read(dve, k, "DN", t)
                        elif e == 0:
                            is_full(dve, k, "DN", t)
                        else:
                            dve.wait_ge(vec_chain, done + 2 * e - half)
                        if e == 0 and half == 1:
                            ins = dve.tensor_scalar(out, part, gate, None, ALU.mult)
                        else:
                            ins = dve.scalar_tensor_tensor(out, part, gate, X[:, t, :] if e == 0 else out, ALU.mult,
                                                           ALU.add)
                        ins.then_inc(vec_chain if t < EARLY or e < E0 // 2 - 1 else read_out[k], 1)
                if t < EARLY:
                    links[0] += E0
                    dve.wait_ge(vec_chain, links[0])
                else:
                    links[0] += E0 - 2
                    for k in banks:
                        is_read(dve, k, "DN", t)
                dve.tensor_tensor(X[:, t, :], sums[0], sums[1], ALU.add).then_inc(experts0_done, 1)

            def two_parts(a, b):
                is_read(dve, TP, "LN", a, b)
                if a == 1 and b > 0:
                    is_full(dve, ST1, "UP0", b - 1, NG * NF - 1)
                elif a == 3 and b == 0:
                    is_full(dve, ST1, "UP0", B - 1, NG * NF - 1)
                elif a == 3:
                    is_full(dve, ST0 + (CH1 - 1) % 2, "UP1", b - 1, CH1 - 1)
                link(dve.tensor_copy(XT_hi[:], XT[:, b, :]))
                dve.tensor_tensor(XT_lo[:], XT[:, b, :], XT_hi[:].bitcast(F32), ALU.subtract)\
                    .then_inc(parts_done[a // 2], 1)

            def logits1(b):
                is_full(dve, PQ, "R1", b)
                lg = bank[PQ][:, 0:TB * R1].rearrange("p (t r) -> p t r", t=TB)
                link(dve.tensor_reduce(m1[:], lg, AX_X, ALU.max))
                dve.tensor_tensor(lg1[:], lg, spread(m1[:], 2, R1), ALU.subtract).then_inc(read_out[PQ], 1)

            def gates1(b):
                dve.wait_ge(e1_done, b + 1)
                p = p1[:, :, 0:R1]
                link(dve.tensor_reduce(s1[:], p, AX_X, ALU.add))
                link(dve.reciprocal(r1[:], s1[:]))
                link(dve.tensor_tensor(p, p, spread(r1[:], 2, R1), ALU.mult))
                for j in range(TB):
                    ins = dve.max(top8[:, j, :], p1[:, j, 0:R1])
                link(ins)
                link(dve.tensor_copy(take8[:, :, 0:TOP1], top8[:, :, 0:TOP1]))
                for j in range(TB):
                    ins = dve.match_replace(rest[:, j, :], take8[:, j, :], p1[:, j, :], 0.0)
                link(ins)
                link(dve.tensor_tensor(gate[:], p, rest[:, :, 0:R1], ALU.subtract))
                link(dve.tensor_copy(g3[:, :, 0, :], gate[:]))
                link(dve.tensor_tensor(gres[:], gate[:], g3[:, :, 0, :], ALU.subtract))
                link(dve.tensor_copy(g3[:, :, 1, :], gres[:]))
                dve.tensor_tensor(g3[:, :, 2, :], gres[:], g3[:, :, 1, :], ALU.subtract).then_inc(g3_done, 1)

            def gates_to_rows(b):
                is_full(dve, TP, "TG", b)
                dve.tensor_copy(gT[0:3 * R1, :], bank[TP][:].bitcast(BF16)[0:3 * R1, 0:S]).then_inc(read_out[TP], 1)

            def gate_hidden(c, b):
                k = SM0 + c % 2
                is_full(dve, k, "GATE", b, c)
                is_read(dve, ST0 + c % 2, "UP1", b, c)
                dve.tensor_tensor(HG[:, c, :], bank[k][:], HG[:, c, :], ALU.mult).then_inc(read_out[k], 1)

            def add_experts1(j, b):
                k = DOWN1_BANKS[j % 2]
                is_full(dve, k, "DN1", b, j)
                t = TB * b + j
                dve.tensor_tensor(X[:, t, :], bank[k][:, 0:D], X[:, t, :], ALU.add).then_inc(read_out[k], 1)

            def mask_to_rows(layer, batches):
                dve.wait_ge(mask_in[layer], 16)
                if layer == 1:
                    is_read(dve, ST1, "ST", 0, B - 1, NC - 1)
                dve.tensor_scalar(shift[64:96, batches, :], mask_i[64:96, :].rearrange("p (b s) -> p b s", b=B)
                                  [:, batches, :], 0.0, MASKED, ALU.is_equal, ALU.mult).then_inc(mask_done[layer], 1)

            def values(layer):
                is_full(dve, PV, "V", layer)
                dve.tensor_tensor(VB[:, layer, :, :].rearrange("p n d -> p (n d)").rearrange("p (b h) -> p b h", b=B),
                                  bank[PV][:].rearrange("p (b h) -> p b h", b=B), spread(bv[layer], 1, B), ALU.add)\
                    .then_inc(read_out[PV], 1)
                is_read(dve, PV, "V", layer)
                dve.tensor_tensor(VB[:, layer, :, :], VB[:, layer, :, :], spread(w("ones_blk"), 1, B * NC), ALU.mult)\
                    .then_inc(vb_done, 1)

            def probabilities():
                for b in range(B):
                    is_read(dve, PQ, "R0", b)
                link(dve.tensor_reduce(lmax[:], LG[:], AX_X, ALU.max))
                dve.tensor_tensor(LG[:], LG[:], spread(lmax[:], 2, E0), ALU.subtract).then_inc(lgs_done, 1)
                dve.wait_ge(e0_done, 1)
                link(dve.tensor_reduce(lsm[:], P0[:], AX_X, ALU.add))
                link(dve.reciprocal(lrc[:], lsm[:]))
                dve.tensor_tensor(P0[:], P0[:], spread(lrc[:], 2, E0), ALU.mult).then_inc(prob_done, 1)
                dve.tensor_copy(same_b[:], w("same_e"))
                dve.tensor_copy(before_b[:], w("before"))
                dve.memset(cand[:], 0)
                dve.wait_ge(tries_in, 16)
                is_full(dve, TP, "P")
                dve.tensor_copy(PRT[:], bank[TP][:, 0:128]).then_inc(read_out[TP], 1)
                is_read(dve, TP, "P")

            def one_digit(i):
                for k in range(TRIES):
                    ins = dve.tensor_scalar((gt, eq, run)[k][:], PRT[:], tries[:, i, k:k + 1].bitcast(F32), None,
                                            ALU.is_ge, ALU.add, accum_out=count[:, k:k + 1])
                ins.then_inc(count_done, 1)
                if 0 < i < DIGITS - 1:
                    link(dve.tensor_tensor(tries[:, i + 1, :], tries[:, i + 1, :],
                                           cand[:].broadcast_to([128, TRIES]), ALU.bitwise_or))
                is_full(dve, PQ, "COUNT", i)
                place = float(1 << (BITS - RADIX_BITS * (i + 1)))
                if RADIX_BITS * (i + 2) <= 24:
                    d = digit_f[:, i % 2:i % 2 + 1]
                    dve.tensor_scalar(reached[:], bank[PQ][:, 0:TRIES], float(TOPK0), None, ALU.is_ge, ALU.add,
                                      accum_out=d).then_inc(read_out[PQ], 1)
                    is_read(dve, PQ, "COUNT", i)
                    dve.scalar_tensor_tensor(tries[:, i + 1, :], d.broadcast_to([128, TRIES]), place,
                                             tries[:, i + 1, :], ALU.mult, ALU.add)
                    link(dve.scalar_tensor_tensor(cand[:], d, place, cand[:], ALU.mult, ALU.add))
                    return
                dve.tensor_scalar(reached[:], bank[PQ][:, 0:TRIES], float(TOPK0), place, ALU.is_ge, ALU.mult)\
                    .then_inc(read_out[PQ], 1)
                is_read(dve, PQ, "COUNT", i)
                d = digit[:, i % 2:i % 2 + 1]
                with nc.allow_low_precision(reason="the sum is a small multiple of a power of two"):
                    link(dve.tensor_reduce(d, reached[:], AX_X, ALU.add))
                if i < DIGITS - 1:
                    dve.tensor_tensor(tries[:, i + 1, :], tries[:, i + 1, :], d.broadcast_to([128, TRIES]),
                                      ALU.bitwise_or)
                link(dve.tensor_tensor(cand[:], cand[:], d, ALU.bitwise_or))

            def take():
                dve.tensor_scalar(gt[:], PRT[:], cand[:].bitcast(F32), None, ALU.is_gt, ALU.add, accum_out=count[:, 0:1])
                link(dve.tensor_scalar(eq[:], PRT[:], cand[:].bitcast(F32), None, ALU.is_equal))
                link(dve.tensor_tensor_scan(run[:], eq[:], eq[:], 0.0, ALU.add, ALU.max))
                dve.tensor_copy(count[:, 1:2], run[:, 127:128]).then_inc(count_done, 1)
                is_full(dve, PQ, "COUNT", DIGITS)
                link(dve.tensor_scalar(left[:, 0:1], bank[PQ][:, 0:1], -1.0, float(TOPK0), ALU.mult, ALU.add))
                dve.tensor_tensor(left[:, 1:2], left[:, 0:1], bank[PQ][:, 1:2], ALU.subtract).then_inc(read_out[PQ], 1)
                is_read(dve, PQ, "COUNT", DIGITS)
                link(dve.scalar_tensor_tensor(eq[:], run[:], left[:, 1:2], eq[:], ALU.is_le, ALU.mult))
                link(dve.tensor_tensor(gt[:], gt[:], eq[:], ALU.add))
                dve.tensor_tensor(GT[:], gt[:], PRT[:], ALU.mult).then_inc(gt_done, 1)

            def gates0():
                is_full(dve, TP, "G")
                dve.tensor_scalar(G0[:].rearrange("p t e -> p (t e)"), bank[TP][:, 0:128], g_tanh[:, 1:2], None, ALU.mult)\
                    .then_inc(read_out[TP], 1)
                is_read(dve, TP, "G")
                mask_to_rows(1, slice(0, B))
                dve.wait_ge(pool_const, TAKE)

            link(dve.memset(shift[:], 0.0))
            dve.wait_ge(w_in[0], 16)
            dve.tensor_copy(ctx4.rearrange("p b (a k) -> p b a k", a=HC),
                            spread(w("ctxT").rearrange("p (b k) -> p b k", b=B), 2, HC)).then_inc(vec_const, 1)
            statistics(0, 0)
            dve.tensor_copy(ident_b[:], ident).then_inc(vec_const, 1)
            for name, a, b in order:
                if name == "LS" and (a, b) != (0, 0):
                    statistics(a, b)
                elif name == "LA":
                    if (a, b) == (0, 0):
                        is_read(dve, PQ, "K", 0)
                        split_keys(dve, 0, link)
                        place_keys(dve, 0, 0, keys_done)
                    normalise(a, b)
                    if a == 0:
                        if b > 0:
                            place_keys(dve, 0, b, keys_done)
                        mask_to_rows(0, slice(b, b + 1))
                elif name == "V":
                    values(a)
                elif name == "Q":
                    queries(a, b)
                elif name == "SM":
                    maxima(a, b)
                elif name == "NT":
                    max_to_rows(a, b)
                    if (a, b) == (0, 0):
                        dve.wait_ge(keep_in, 16)
                        link(dve.tensor_scalar(keep_f[:], keep_i[:], 0.0, None, ALU.not_equal))
                        link(dve.tensor_reduce(any_keep[:], keep_f[:], AX_X, ALU.max))
                elif name == "WG":
                    weigh(a, b)
                elif name == "O":
                    add_attention(a, b)
                elif name == "R0":
                    is_full(dve, PQ, "R0", b)
                    dve.tensor_tensor(LG[:, TB * b:TB * b + TB, :],
                                      bank[PQ][:, 0:TB * E0].rearrange("p (t e) -> p t e", t=TB),
                                      spread(rows[:, 2 * D:2 * D + E0], 1, TB), ALU.add).then_inc(read_out[PQ], 1)
                elif name == "RP":
                    probabilities()
                elif name == "CT":
                    if a < DIGITS:
                        one_digit(a)
                    else:
                        take()
                elif name == "GT":
                    gates0()
                elif name == "BD":
                    combine(a, b)
                elif name == "XL":
                    two_parts(a, b)
                elif name == "R1":
                    logits1(b)
                elif name == "GA":
                    gates1(b)
                elif name == "TG":
                    gates_to_rows(b)
                elif name == "SG":
                    gate_hidden(a, b)
                elif name == "DN1":
                    add_experts1(a, b)


_INS = ["x", "mask_tm", "mask_t", "weights", "tries_of", "gates", "w_up", "b_up", "w_down", "b_down", "w_up1", "w_dn1"]


def kernel(x, ctx_1024, mask_BxSxS2_if1, mask_BxSxS2_ik0, g_xattn, g_ffn, L0_xattn_Wq, L0_xattn_bq, L0_xattn_Wk,
           L0_xattn_bk, L0_xattn_Wv, L0_xattn_bv, L0_xattn_Wo, L0_xattn_bo, L0_ffn_Wr, L0_ffn_br, L0_ffn_W_up,
           L0_ffn_b_up, L0_ffn_W_down, L0_ffn_b_down, L1_xattn_W_kv, L1_xattn_b_kv, L1_xattn_W_q, L1_xattn_b_q,
           L1_xattn_W_o, L1_xattn_b_o, L1_ffn_shared_up, L1_ffn_shared_down, L1_ffn_routed_up, L1_ffn_routed_down,
           L1_ffn_router_w):
    import numpy as np
    import concourse.bacc as bacc
    from concourse.bass_utils import run_bass_kernel_spmd

    def on_rows(v):
        return np.broadcast_to(np.asarray(v).reshape(1, -1), (128, np.asarray(v).size))

    wkv = np.asarray(L1_xattn_W_kv).reshape(D, H, 2, DK)
    bkv = np.asarray(L1_xattn_b_kv).reshape(H, 2, DK)
    p, c = np.arange(128)[:, None], np.arange(128)[None, :]
    f32 = np.float32
    parts = {
        "wq0": np.asarray(L0_xattn_Wq).T, "wk0": np.asarray(L0_xattn_Wk).T, "wv0": np.asarray(L0_xattn_Wv).T,
        "wo0": np.asarray(L0_xattn_Wo).T, "ctxT": np.asarray(ctx_1024).reshape(B * SK, D).T,
        "wk1": wkv[:, :, 0].reshape(D, D), "wv1": wkv[:, :, 1].reshape(D, D), "wq1": np.asarray(L1_xattn_W_q),
        "wo1": np.asarray(L1_xattn_W_o), "wr0": np.asarray(L0_ffn_Wr), "wr1": np.asarray(L1_ffn_router_w).T,
        "cols": np.stack([np.asarray(L0_xattn_bq), np.asarray(L0_xattn_bk), np.asarray(L1_xattn_b_q),
                          bkv[:, 0].reshape(D)], 1),
        "rows": np.concatenate([on_rows(L0_xattn_bo), on_rows(L1_xattn_b_o), on_rows(L0_ffn_br),
                                on_rows(L0_xattn_bv), on_rows(bkv[:, 1].reshape(D))], 1),
        "ident": (p == c).astype(f32),
        "same_e": (p % E0 == c % E0).astype(f32),
        "before": ((p % E0 == c % E0) & (p // E0 < c // E0)).astype(f32),
        "headcol": (p // DK == c[:, :H]).astype(f32),
        "ones_blk": (p // SK == c[:, :HC * DK] // DK).astype(f32),
        "key32": (p - 64 == c[:, :SK]).astype(f32),
        "max16": ((p < 2 * H) & (p % H == c[:, :H])).astype(f32),
        "gate16": ((p < 3 * R1) & (p % R1 == c[:, :R1])).astype(f32),
    }
    digit = np.arange(DIGITS)[:, None]
    tries_of = on_rows((np.arange(1, TRIES + 1)[None, :] << (BITS - RADIX_BITS * (digit + 1))).astype(np.int32))
    weights = np.concatenate([parts[n] for n in W_COLS], 1)
    b_up = np.zeros((128, NG, NF), f32)
    for k, (f0, fn) in enumerate(FCH):
        b_up[:fn, :, k] = np.asarray(L0_ffn_b_up)[:, f0:f0 + fn].T
    up1 = np.concatenate([np.asarray(L1_ffn_routed_up).reshape(R1 * EH, D),
                          np.asarray(L1_ffn_shared_up).reshape(-1, D)]).T
    dn1 = np.concatenate([np.asarray(L1_ffn_routed_down).transpose(0, 2, 1).reshape(R1 * EH, D),
                          np.asarray(L1_ffn_shared_down).transpose(0, 2, 1).reshape(-1, D)])
    masks = [np.asarray(m).reshape(B * S, SK) for m in (mask_BxSxS2_if1, mask_BxSxS2_ik0)]
    gx, gf = np.asarray(g_xattn), np.asarray(g_ffn)
    given = {
        "x": np.asarray(x).reshape(B * S, D), "mask_tm": masks[0], "mask_t": np.stack([m.T for m in masks]),
        "weights": weights, "tries_of": tries_of, "gates": on_rows(np.stack([gx[0], gf[0], gx[1], gf[1]])),
        "w_up": np.asarray(L0_ffn_W_up), "b_up": b_up, "w_down": np.asarray(L0_ffn_W_down),
        "b_down": np.asarray(L0_ffn_b_down), "w_up1": up1,
        "w_dn1": dn1.reshape(CH1, 128, D).transpose(1, 0, 2),
    }
    nc = bacc.Bacc("TRN2", target_bir_lowering=False, num_devices=1)
    arrays, args = {}, []
    for name in _INS:
        a = np.ascontiguousarray(given[name])
        arrays[f"in_{name}"] = a
        args.append(nc.dram_tensor(f"in_{name}", a.shape, mybir.dt.from_np(a.dtype), kind="ExternalInput").ap())
    args.append(nc.dram_tensor("out_x", (B * S, D), F32, kind="ExternalOutput").ap())
    build(nc, *args)
    r = run_bass_kernel_spmd(nc, [arrays], core_ids=[0])
    return r.results[0]["out_x"].reshape(B, S, D)
```
